# Optimizing a Trainium2 kernel written in Bass

```python
import numpy as np
import jax
import jax.numpy as jnp

def _softmax(x, axis=-1):
    return jax.nn.softmax(x, axis=axis)

def _gelu(x):
    return jax.nn.gelu(x, approximate=True)

def _silu(x):
    return jax.nn.silu(x)

def _sigmoid(x):
    return jax.nn.sigmoid(x)

def _layernorm(x, axis=-1, eps=1e-05):
    m = jnp.mean(x, axis=axis, keepdims=True)
    v = jnp.var(x, axis=axis, keepdims=True)
    return (x - m) / jnp.sqrt(v + eps)

def _scatter_add(tgt, idx, src, axis=0):
    return tgt.at[idx].add(src)

def _segment_sum(src, seg, n):
    return jax.ops.segment_sum(src, seg, n)
kernel_name = 'mk_gnn_resnorm_d4_gnn_r64_851eb8'

def setup_inputs(seed: int=0):
    np.random.seed(seed)
    _w = jnp.asarray

    def _rec_inputs():
        import jax
        import jax.numpy as jnp
        _gk = jax.random.key(seed)
        x = -0.0003713 + 1 * jax.random.normal(jax.random.fold_in(_gk, 1), (100000, 128), jnp.float32)
        src = jax.random.randint(jax.random.fold_in(_gk, 2), (50000,), 0, 100000, jnp.int32)
        dst = jax.random.randint(jax.random.fold_in(_gk, 3), (50000,), 0, 100000, jnp.int32)
        _o = jnp.argsort(dst, stable=True)
        src = src[_o]
        dst = dst[_o]
        edge_attr_20 = -9.88767e-05 + 0.999954 * jax.random.normal(jax.random.fold_in(_gk, 12), (50000, 20), jnp.float32)
        edge_weight = jax.random.uniform(jax.random.fold_in(_gk, 14), (50000,), jnp.float32, 0.0, 0.999998)
        return (x, src, dst, edge_attr_20, edge_weight)
    x, src, dst, edge_attr_20, edge_weight = _rec_inputs()

    def _L0_gnn_setup():
        import jax, jax.numpy as jnp
        import numpy as np
        N = 100000
        E = 25000
        D = 128

        def _sage_mean(x, src, dst, W_self, b_self, W_neigh):
            msg = x[src]
            ssum = jax.ops.segment_sum(msg, dst, num_segments=N)
            deg = jax.ops.segment_sum(jnp.ones((src.shape[0],), x.dtype), dst, num_segments=N)
            neigh = jnp.where(deg[:, None] > 0, ssum / jnp.maximum(deg, 1.0)[:, None], 0.0)
            return x @ W_self.T + b_self + neigh @ W_neigh.T
        key = jax.random.key(seed)
        ks = jax.random.split(key, 8)
        h = jax.random.normal(ks[0], (N, D), dtype=jnp.float32)
        src = jax.random.randint(ks[1], (E,), 0, N)
        dst = jax.random.randint(ks[2], (E,), 0, N)
        gain = float(np.sqrt(2.0))
        bound = gain * float(np.sqrt(6.0 / (D + D)))

        def w(k):
            return jax.random.uniform(k, (D, D), jnp.float32, -bound, bound)
        return {'h': h, 'src': src, 'dst': dst, 'W_self0': w(ks[3]), 'b_self0': jnp.zeros((D,), jnp.float32), 'W_neigh0': w(ks[4]), 'W_self1': w(ks[5]), 'b_self1': jnp.zeros((D,), jnp.float32), 'W_neigh1': w(ks[6])}
    _L0_gnn_all = _L0_gnn_setup()
    _L0_gnn_in = {k: v for k, v in _L0_gnn_all.items() if k in ('W_self0', 'b_self0', 'W_neigh0', 'W_self1', 'b_self1', 'W_neigh1')}
    del _L0_gnn_all

    def _L1_gnn_setup():
        import jax, jax.numpy as jnp
        import numpy as np
        EPS = 1e-07
        N_NODES, N_EDGES, D = (10000, 2500, 128)

        def mobius_add(x, y):
            x2 = jnp.sum(x * x, axis=-1, keepdims=True)
            y2 = jnp.sum(y * y, axis=-1, keepdims=True)
            xy = jnp.sum(x * y, axis=-1, keepdims=True)
            num = (1.0 + 2.0 * xy + y2) * x + (1.0 - x2) * y
            den = 1.0 + 2.0 * xy + x2 * y2
            return num / jnp.maximum(den, EPS)

        def mobius_scalar_mul(r, x):
            nrm = jnp.sqrt(jnp.sum(x * x, axis=-1, keepdims=True))
            nrm_c = jnp.clip(nrm, EPS, 1.0 - EPS)
            scaled = jnp.tanh(r * jnp.arctanh(nrm_c)) * (x / nrm_c)
            return jnp.where(nrm > EPS, scaled, jnp.zeros_like(x))
        key = jax.random.key(seed)
        kx, ke = jax.random.split(key)
        raw = jax.random.normal(kx, (N_NODES, D), dtype=jnp.float32)
        x = 0.4 * raw / (1.0 + jnp.linalg.norm(raw, axis=-1, keepdims=True))
        edge_index = jax.random.randint(ke, (2, N_EDGES), 0, N_NODES, dtype=jnp.int64)
        return {'x': x, 'edge_index': edge_index}
    _L1_gnn_all = _L1_gnn_setup()
    _L1_gnn_in = {k: v for k, v in _L1_gnn_all.items() if k in ()}
    del _L1_gnn_all

    def _L2_gnn_setup():
        import jax, jax.numpy as jnp
        import numpy as np
        LOG2 = 0.6931471805599453

        def shifted_softplus(x):
            return jax.nn.softplus(x) - LOG2
        N_ATOMS = 20000
        N_EDGES = 9375
        N_BASIS = 128
        N_RBF = 20
        N_FILT = 128
        key = jax.random.key(seed)
        ks = jax.random.split(key, 12)
        s = lambda k, sh, fan_in: jax.random.normal(k, sh, jnp.float32) / np.sqrt(fan_in)
        return {'x': jax.random.normal(ks[0], (N_ATOMS, N_BASIS), jnp.float32), 'f_ij': jax.random.normal(ks[1], (N_EDGES, N_RBF), jnp.float32), 'idx_i': jax.random.randint(ks[2], (N_EDGES,), 0, N_ATOMS), 'idx_j': jax.random.randint(ks[3], (N_EDGES,), 0, N_ATOMS), 'rcut_ij': jax.random.uniform(ks[4], (N_EDGES,), jnp.float32), 'W_in2f': s(ks[5], (N_FILT, N_BASIS), N_BASIS), 'b_in2f': jnp.zeros((N_FILT,), jnp.float32), 'W_f1': s(ks[6], (N_FILT, N_RBF), N_RBF), 'b_f1': jnp.zeros((N_FILT,), jnp.float32), 'W_f2': s(ks[7], (N_FILT, N_FILT), N_FILT), 'b_f2': jnp.zeros((N_FILT,), jnp.float32), 'W_o1': s(ks[8], (N_BASIS, N_FILT), N_FILT), 'b_o1': jnp.zeros((N_BASIS,), jnp.float32), 'W_o2': s(ks[9], (N_BASIS, N_BASIS), N_BASIS), 'b_o2': jnp.zeros((N_BASIS,), jnp.float32)}
    _L2_gnn_all = _L2_gnn_setup()
    _L2_gnn_in = {k: v for k, v in _L2_gnn_all.items() if k in ('W_in2f', 'b_in2f', 'W_f1', 'b_f1', 'W_f2', 'b_f2', 'W_o1', 'b_o1', 'W_o2', 'b_o2')}
    del _L2_gnn_all

    def _L3_gnn_setup():
        import jax, jax.numpy as jnp
        import numpy as np
        N_NODES, N_EDGES, D_IN, D_OUT = (50000, 12500, 128, 128)
        key = jax.random.key(seed)
        k1, k2, k3, k4 = jax.random.split(key, 4)
        h = jax.random.normal(k1, (N_NODES, D_IN), dtype=jnp.float32)
        src = jax.random.randint(k2, (N_EDGES,), 0, N_NODES)
        dst = jax.random.randint(k3, (N_EDGES,), 0, N_NODES)
        W = jax.random.normal(k4, (2 * D_IN, D_OUT), dtype=jnp.float32) * 0.05
        b = jnp.zeros((D_OUT,), dtype=jnp.float32)
        return {'h': h, 'src': src, 'dst': dst, 'W': W, 'b': b}
    _L3_gnn_all = _L3_gnn_setup()
    _L3_gnn_in = {k: v for k, v in _L3_gnn_all.items() if k in ('W', 'b')}
    del _L3_gnn_all
    return {'x': x, 'src': src, 'dst': dst, 'edge_attr_20': edge_attr_20, 'edge_weight': edge_weight, 'L0_gnn_W_self0': _L0_gnn_in['W_self0'], 'L0_gnn_b_self0': _L0_gnn_in['b_self0'], 'L0_gnn_W_neigh0': _L0_gnn_in['W_neigh0'], 'L0_gnn_W_self1': _L0_gnn_in['W_self1'], 'L0_gnn_b_self1': _L0_gnn_in['b_self1'], 'L0_gnn_W_neigh1': _L0_gnn_in['W_neigh1'], 'L2_gnn_W_in2f': _L2_gnn_in['W_in2f'], 'L2_gnn_b_in2f': _L2_gnn_in['b_in2f'], 'L2_gnn_W_f1': _L2_gnn_in['W_f1'], 'L2_gnn_b_f1': _L2_gnn_in['b_f1'], 'L2_gnn_W_f2': _L2_gnn_in['W_f2'], 'L2_gnn_b_f2': _L2_gnn_in['b_f2'], 'L2_gnn_W_o1': _L2_gnn_in['W_o1'], 'L2_gnn_b_o1': _L2_gnn_in['b_o1'], 'L2_gnn_W_o2': _L2_gnn_in['W_o2'], 'L2_gnn_b_o2': _L2_gnn_in['b_o2'], 'L3_gnn_W': _L3_gnn_in['W'], 'L3_gnn_b': _L3_gnn_in['b']}

def reference(x, src, dst, edge_attr_20, edge_weight, L0_gnn_W_self0, L0_gnn_b_self0, L0_gnn_W_neigh0, L0_gnn_W_self1, L0_gnn_b_self1, L0_gnn_W_neigh1, L2_gnn_W_in2f, L2_gnn_b_in2f, L2_gnn_W_f1, L2_gnn_b_f1, L2_gnn_W_f2, L2_gnn_b_f2, L2_gnn_W_o1, L2_gnn_b_o1, L2_gnn_W_o2, L2_gnn_b_o2, L3_gnn_W, L3_gnn_b):
    import jax
    import jax.numpy as jnp

    def _L0_gnn_ref(h, src, dst, W_self0, b_self0, W_neigh0, W_self1, b_self1, W_neigh1):
        import jax, jax.numpy as jnp
        import numpy as np
        N = 100000
        E = 25000
        D = 128

        def _sage_mean(x, src, dst, W_self, b_self, W_neigh):
            msg = x[src]
            ssum = jax.ops.segment_sum(msg, dst, num_segments=N)
            deg = jax.ops.segment_sum(jnp.ones((src.shape[0],), x.dtype), dst, num_segments=N)
            neigh = jnp.where(deg[:, None] > 0, ssum / jnp.maximum(deg, 1.0)[:, None], 0.0)
            return x @ W_self.T + b_self + neigh @ W_neigh.T
        t1 = _sage_mean(h, src, dst, W_self0, b_self0, W_neigh0)
        t2 = _sage_mean(t1, src, dst, W_self1, b_self1, W_neigh1)
        return h + t1 + t2 * 0.5

    def _L1_gnn_ref(x, edge_index):
        import jax, jax.numpy as jnp
        import numpy as np
        EPS = 1e-07
        N_NODES, N_EDGES, D = (10000, 2500, 128)

        def mobius_add(x, y):
            x2 = jnp.sum(x * x, axis=-1, keepdims=True)
            y2 = jnp.sum(y * y, axis=-1, keepdims=True)
            xy = jnp.sum(x * y, axis=-1, keepdims=True)
            num = (1.0 + 2.0 * xy + y2) * x + (1.0 - x2) * y
            den = 1.0 + 2.0 * xy + x2 * y2
            return num / jnp.maximum(den, EPS)

        def mobius_scalar_mul(r, x):
            nrm = jnp.sqrt(jnp.sum(x * x, axis=-1, keepdims=True))
            nrm_c = jnp.clip(nrm, EPS, 1.0 - EPS)
            scaled = jnp.tanh(r * jnp.arctanh(nrm_c)) * (x / nrm_c)
            return jnp.where(nrm > EPS, scaled, jnp.zeros_like(x))
        src, dst = (edge_index[0], edge_index[1])
        n, d = x.shape
        messages = mobius_add(x[src], -x[dst])

        def body(out, em):
            m, idx = em
            return (out.at[idx].set(mobius_add(out[idx], m)), None)
        out0 = jnp.zeros((n, d), dtype=x.dtype)
        total, _ = jax.lax.scan(body, out0, (messages, dst))
        count = jnp.zeros((n,), dtype=x.dtype).at[dst].add(1.0)
        scale = 1.0 / jnp.maximum(count, 1.0)
        aggr = mobius_scalar_mul(scale[:, None], total)
        return mobius_add(x, aggr)

    def _L2_gnn_ref(x, f_ij, idx_i, idx_j, rcut_ij, W_in2f, b_in2f, W_f1, b_f1, W_f2, b_f2, W_o1, b_o1, W_o2, b_o2):
        import jax, jax.numpy as jnp
        import numpy as np
        LOG2 = 0.6931471805599453

        def shifted_softplus(x):
            return jax.nn.softplus(x) - LOG2
        N_ATOMS = 20000
        N_EDGES = 9375
        N_BASIS = 128
        N_RBF = 20
        N_FILT = 128
        n_atoms = x.shape[0]
        h = x @ W_in2f.T + b_in2f
        Wij = shifted_softplus(f_ij @ W_f1.T + b_f1)
        Wij = Wij @ W_f2.T + b_f2
        Wij = Wij * rcut_ij[:, None]
        x_ij = h[idx_j] * Wij
        agg = jax.ops.segment_sum(x_ij, idx_i, num_segments=n_atoms)
        out = shifted_softplus(agg @ W_o1.T + b_o1)
        out = out @ W_o2.T + b_o2
        return out

    def _L3_gnn_ref(h, src, dst, W, b):
        import jax, jax.numpy as jnp
        import numpy as np
        N_NODES, N_EDGES, D_IN, D_OUT = (50000, 12500, 128, 128)
        N = h.shape[0]
        msgs = h[src]
        s = jax.ops.segment_sum(msgs, dst, num_segments=N)
        deg = jax.ops.segment_sum(jnp.ones(src.shape, h.dtype), dst, num_segments=N)
        c = s / jnp.maximum(deg, 1.0)[:, None]
        new_h = jax.nn.relu(jnp.concatenate([h, c], axis=-1) @ W + b)
        return jnp.where((deg > 0)[:, None], new_h, h)
    edge_index = jnp.stack([src, dst])
    x = _layernorm(x + _L0_gnn_ref(x, src, dst, L0_gnn_W_self0, L0_gnn_b_self0, L0_gnn_W_neigh0, L0_gnn_W_self1, L0_gnn_b_self1, L0_gnn_W_neigh1), axis=-1)
    x = _layernorm(x + _L1_gnn_ref(x, edge_index), axis=-1)
    x = _layernorm(x + _L2_gnn_ref(x, edge_attr_20, src, dst, edge_weight, L2_gnn_W_in2f, L2_gnn_b_in2f, L2_gnn_W_f1, L2_gnn_b_f1, L2_gnn_W_f2, L2_gnn_b_f2, L2_gnn_W_o1, L2_gnn_b_o1, L2_gnn_W_o2, L2_gnn_b_o2), axis=-1)
    x = _layernorm(x + _L3_gnn_ref(x, src, dst, L3_gnn_W, L3_gnn_b), axis=-1)
    return x

_drawn_inputs = setup_inputs


def setup_inputs(seed=0):
    import zlib

    import numpy as np

    out = dict(_drawn_inputs(seed))
    spreads = {'L0_gnn_b_self0': (0.0, 0.1),
     'L0_gnn_b_self1': (0.0, 0.477),
     'L2_gnn_b_in2f': (0.0, 0.8),
     'L2_gnn_b_f1': (0.0, 0.725),
     'L2_gnn_b_f2': (0.0, 0.368),
     'L2_gnn_b_o1': (0.0, 0.1),
     'L2_gnn_b_o2': (0.0, 0.1),
     'L3_gnn_b': (0.0, 0.1)}
    factors = {}
    for name, (base, spread) in spreads.items():
        noise = np.random.default_rng([zlib.crc32(name.encode()), seed]).standard_normal(out[name].shape)
        drawn = base * np.exp(spread * noise) if base else spread * noise
        out[name] = jnp.asarray(drawn.astype(out[name].dtype))
    for name, factor in factors.items():
        out[name] = (out[name] * factor).astype(out[name].dtype)
    return out
```

```python
from contextlib import ExitStack

import concourse.bass as bass
from concourse import mybir

P = 128
D = 128
N = 100000
E = 50000

G = 4
S = 7
LANES = P * G
C = S * -(-E // (LANES * S))
MAIN = C // S
TAIL_MAX = E // S + 1
FIELDS = 5
SRC, OUT, CONT, RDEG, DST = range(FIELDS)
PARTS = ((SRC, OUT + 1), (CONT, RDEG + 1), (DST, DST + 1))
E_PAD = LANES * C + C + S * (TAIL_MAX + 1)

NB = 4
BN = P * NB
BATCHES = -(-N // BN)
NP = BATCHES * BN
SN = 4
WITH = BATCHES // C
assert WITH * C == BATCHES

JG = 4
GE = P * JG
SG = 4
GROUPS = SG * -(-E // (GE * SG))
RBF = 20
DUMMY = NP
AGG_ROWS = NP + GE + 1

EPS_LN = 1e-5
EPS = 1e-7
ONE_MINUS_SQ = float.fromhex("0x1.fffff8p-1")

F32 = mybir.dt.float32
I32 = mybir.dt.int32
ALU = mybir.AluOpType
ACT = mybir.ActivationFunctionType
AX = mybir.AxisListType.X
RED = bass.bass_isa.ReduceOp

CREDIT = 8


def done(t):
    return t + 1 + CREDIT


def freed(t, k):
    return t + 1 + CREDIT - k


def pipeline(blocks, slots, eng, stages, main=None):
    depth = max(stage[0] for stage in stages)
    every = [stage for stage in stages if len(stage) == 2]
    assert depth <= slots
    for u in range(slots):
        for d, f, *_ in stages:
            if u >= d:
                f(0, u - d)
    if main is not None:
        with eng.Fori(1, main) as b:
            for u in range(slots):
                for d, f, *_ in stages:
                    f(b if u >= d else b - 1, (u - d) % slots)
    with eng.Fori(1 if main is None else main, blocks) as b:
        for u in range(slots):
            for d, f in every:
                f(b if u >= d else b - 1, (u - d) % slots)
    for u in range(depth):
        for d, f in every:
            if u < d:
                f(blocks - 1, (u - d) % slots)


def held(eng, sem, value, hold):
    eng.wait_ge(sem, value)
    eng.sem_inc(hold, 1)


class Steps:

    def __init__(self, eng, sem):
        self.eng, self.sem, self.n = eng, sem, 0

    def do(self, ins):
        ins.then_inc(self.sem, 1)
        self.n += 1

    def settle(self):
        if self.n:
            self.eng.wait_ge(self.sem, self.n)

    def step(self, ins):
        self.do(ins)
        self.settle()

    def restart(self):
        if self.n:
            self.settle()
            self.eng.sem_clear(self.sem)
            self.n = 0


def lanes_of(v, n):
    return v.rearrange("p (g o) -> p g o", o=1).to_broadcast([P, n, D])


def over_rows(v, n):
    return v.rearrange("p (o d) -> p o d", o=1).to_broadcast([P, n, D])


def flat(t):
    return t[:].rearrange("p r d -> p (r d)")


def blocks_of(eng, tail):
    return eng.value_load(tail[0:1, 0:1], min_val=1, max_val=TAIL_MAX + 1) + MAIN


ZC = 2048


def clear_table(eng, table, zeros, cleared):
    line = table.rearrange("n d -> (n d)")
    total, at, count = table.shape[0] * table.shape[1], 0, 0
    while at < total:
        n = min(P * ZC, total - at)
        n -= n % P if n > P else 0
        eng.dma_start(line[at:at + n].rearrange("(p c) -> p c", p=P), zeros[:, 0:n // P]).then_inc(cleared, 16)
        at += n
        count += 1
    return count


def gnn_kernel(nc, a, out):
    x = a["x"]
    with ExitStack() as whole:
        def keep(name, shape, dt=F32):
            return whole.enter_context(nc.sbuf_tensor(name, shape, dt))

        meta = [nc.dram_tensor(f"meta{lo}", [S * (MAIN + TAIL_MAX + 1), P, (hi - lo) * G], I32, kind="Internal").ap()
                for lo, hi in PARTS]
        t_mean, t_part, t_z, x1, x2, x3 = (
            nc.dram_tensor(n, [NP, D], F32, kind="Internal").ap() for n in ("t_mean", "t_part", "t_z", "x1", "x2", "x3"))
        t_agg = nc.dram_tensor("t_agg", [AGG_ROWS, D], F32, kind="Internal").ap()

        zeros = keep("zeros", [P, ZC])
        ident = keep("ident", [P, P])
        consts = keep("consts", [P, 4])
        half, one = consts[:, 2:3], consts[:, 1:2]
        tail = keep("tail", [P, 1], I32)
        w = {n: keep("w_" + n, [P, D]) for n in ("g0", "g1", "g2", "c", "g", "in2f", "f2", "o1", "o2", "h3", "c3")}
        w_f1 = keep("w_f1", [RBF, D])
        col = keep("col", [P, 2])
        bias3 = keep("bias3", [P, D])
        rows = keep("rows", [1, 3, BN])
        ones_row = keep("ones_row", [1, P])

        prepare(nc, a, meta, zeros, t_mean, ident, consts, tail, w, w_f1, col, rows, bias3, ones_row)
        mean_pass(nc, meta, tail, x, t_mean, zeros, (t_z, t_agg))
        second_mean_pass(nc, meta, tail, x, t_mean, t_part, t_z, ident, w)
        sage_nodes(nc, t_part, t_z, x1, x2)
        mobius_pass(nc, meta, tail, x1, x2, consts)
        schnet_edges(nc, a, x2, t_agg, ident, w, w_f1, col, rows, ones_row, half, one)
        schnet_nodes(nc, x2, t_agg, x3, out, ident, w, col, rows, ones_row, half)
        last_pass(nc, meta, tail, x3, out, ident, w, bias3, consts)


def prepare(nc, a, meta, zeros, t_mean, ident, consts, tail, w, w_f1, col, rows, bias3, ones_row):
    with ExitStack() as ctx:
        sems = []
        ctx.callback(nc.all_engine_barrier)
        ctx.callback(nc.clear_and_free_semaphores, sems)

        def sb(name, shape, dt=F32):
            return ctx.enter_context(nc.sbuf_tensor(name, shape, dt))

        def sem(name):
            sems.append(nc.alloc_semaphore("pre_" + name))
            return sems[-1]

        raw = {n: sb("raw_" + n, [P, D]) for n in ("s0", "n0", "s0t", "n0t", "s1t", "n1t")}
        bcol = sb("bcol", [P, 1])
        brow0 = sb("brow0", [P, D])
        brow1 = sb("brow1", [P, D])
        bwide = sb("bwide", [P, P])
        tmp = sb("tmp", [P, D])
        dwin = sb("dwin", [P, G, C + 2], I32)
        swin = sb("swin", [P, G, C], I32)
        W = sb("W", [P, G, C + 2])
        NS = sb("NS", [P, G, C + 1])
        SM = sb("SM", [P, G, C + 1])
        V, A, T1, RK, T2 = (sb(n, [P, G, C]) for n in ("V", "A", "T1", "RK", "T2"))
        msb = sb("msb", [P, C, FIELDS, G], I32)
        msf = msb[:].bitcast(F32)
        lanes = sb("lanes", [P, 2, G])
        lead = sb("lead", [P, 2])
        allr = sb("allr", [P, 2])
        tl = sb("tl", [P, 1], I32)
        dwt = sb("dwt", [P, G, S + 2], I32)
        swt = sb("swt", [P, G, S], I32)
        Wt = sb("Wt", [P, G, S + 2])
        NSt = sb("NSt", [P, G, S + 1])
        SMt = sb("SMt", [P, G, S + 1])
        Vt, At, T1t, RKt, T2t = (sb(n, [P, G, S]) for n in ("Vt", "At", "T1t", "RKt", "T2t"))
        mst = sb("mst", [P, S, FIELDS, G], I32)
        mstf = mst[:].bitcast(F32)
        carry = sb("carry", [P, 2, G])
        ps = [ctx.enter_context(nc.psum_tensor(f"pre_ps{k}", [P, 512], F32)) for k in range(4)]

        s_w = sem("weights")
        s_win = sem("window")
        s_zero = sem("zeros")
        s_zeroed = sem("zeroed")
        s_dve = sem("dve")
        s_prod = sem("prod")
        s_wide = sem("wide")
        s_meta = sem("meta")
        s_meta_out = sem("meta_out")
        s_lead = sem("lead")
        s_red = sem("red")
        s_tail = sem("tail")
        s_twin = sem("tail_window")
        s_tmeta = sem("tail_meta")
        s_tout = sem("tail_out")
        s_pool = sem("pool")
        s_hold = sem("hold")

        def window(arr, off, lo, hi):
            return arr[bass.ds(off, LANES * C)].rearrange("(p g c) -> p g c", g=G, c=C)[:, :, lo:hi]

        block = ctx.enter_context(nc.Block())

        @block.sync
        def _(sp):
            sp.dma_start(dwin[:, :, 0:C], window(a["dst_pad"], 0, 0, C)).then_inc(s_win, 16)
            sp.dma_start(dwin[:, :, C:C + 2], window(a["dst_pad"], C, 0, 2)).then_inc(s_win, 16)
            sp.dma_start(swin[:], window(a["src_pad"], 0, 0, C)).then_inc(s_win, 16)
            for n in ("s0", "n0", "s0t", "n0t", "s1t", "n1t"):
                sp.dma_start(raw[n][:], a[n]).then_inc(s_w, 16)
            sp.dma_start(bcol[:], a["b_self0"].rearrange("(p o) -> p o", o=1)).then_inc(s_w, 16)
            sp.dma_start(brow0[:], a["b_self0"].rearrange("(o d) -> o d", o=1).to_broadcast([P, D])).then_inc(s_w, 16)
            sp.dma_start(brow1[:], a["b_self1"].rearrange("(o d) -> o d", o=1).to_broadcast([P, D])).then_inc(s_w, 16)
            for n in ("in2f", "f2", "o1", "o2", "h3", "c3"):
                sp.dma_start(w[n][:], a["w_" + n]).then_inc(s_w, 16)
            sp.dma_start(w_f1[:], a["w_f1"]).then_inc(s_w, 16)
            sp.dma_start(col[:, 0:1], a["b_f1"].rearrange("(p o) -> p o", o=1)).then_inc(s_w, 16)
            sp.dma_start(col[:, 1:2], a["b_o1"].rearrange("(p o) -> p o", o=1)).then_inc(s_w, 16)
            sp.dma_start(bias3[:], a["b_3"].rearrange("(o d) -> o d", o=1).to_broadcast([P, D])).then_inc(s_w, 16)
            for k, n in enumerate(("b_in2f", "b_f2", "b_o2")):
                sp.dma_start(rows[0:1, k, :], a[n].rearrange("(o r d) -> o r d", o=1, r=1).to_broadcast([1, NB, D])).then_inc(s_w, 16)
            held(sp, s_meta, 1, s_hold)
            for part, (lo, hi) in zip(meta, PARTS):
                sp.dma_start(part[0:C].rearrange("s p f -> p s f"),
                             msb[:, :, lo:hi, :].rearrange("p s f g -> p s (f g)")).then_inc(s_meta_out, 16)
            held(sp, s_tail, 1, s_hold)
            k_tail = sp.value_load(tail[0:1, 0:1], min_val=1, max_val=TAIL_MAX + 1)
            sp.sem_inc(s_tout, CREDIT)
            with sp.Fori(0, k_tail) as k:
                held(sp, s_tmeta, k + CREDIT, s_hold)
                sp.dma_start(dwt[:], window(a["dst_pad"], C + k * S, 0, S + 2)).then_inc(s_twin, 16)
                sp.dma_start(swt[:], window(a["src_pad"], C + k * S, 0, S)).then_inc(s_twin, 16)
                held(sp, s_tmeta, k + 1 + CREDIT, s_hold)
                for part, (lo, hi) in zip(meta, PARTS):
                    sp.dma_start(part[bass.ds(C + S * k, S)].rearrange("s p f -> p s f"),
                                 mst[:, :, lo:hi, :].rearrange("p s f g -> p s (f g)")).then_inc(s_tout, 16)
                held(sp, s_tout, k * 48 + 48 + CREDIT, s_hold)
            held(sp, s_meta_out, 48, s_hold)
            held(sp, s_w, 16 * 22, s_hold)

        @block.scalar
        def _(act):
            act.preload_act_table_set("natural_log_exp_and_others")
            act.wait_ge(s_zero, 1)
            count = clear_table(act, t_mean, zeros, s_zeroed)
            act.wait_ge(s_zeroed, 16 * count)

        @block.gpsimd
        def _(pool):
            pool.memset(ident[:], 0.0).then_inc(s_pool, 1)
            held(pool, s_pool, 1, s_hold)
            pool.affine_select(out=ident[:], in_=ident[:], compare_op=ALU.not_equal, fill=1.0, base=0,
                               pattern=[[-1, P]], channel_multiplier=1).then_inc(s_pool, 1)
            held(pool, s_lead, 1, s_hold)
            pool.partition_all_reduce(allr[:, 0:1], lead[:, 0:1], P, RED.max).then_inc(s_red, 1)
            pool.partition_all_reduce(allr[:, 1:2], lead[:, 1:2], P, RED.add).then_inc(s_red, 1)

        @block.tensor
        def _(pe):
            pe.wait_ge(s_w, 16 * 22)
            pe.matmul(ps[0][:, 0:D], raw["s0"][:], raw["s1t"][:], start=True, stop=True).then_inc(s_prod, 1)
            pe.matmul(ps[1][:, 0:D], raw["n0"][:], raw["s1t"][:], start=True, stop=False)
            pe.matmul(ps[1][:, 0:D], raw["s0"][:], raw["n1t"][:], start=False, stop=True).then_inc(s_prod, 1)
            pe.matmul(ps[2][:, 0:D], raw["n0"][:], raw["n1t"][:], start=True, stop=True).then_inc(s_prod, 1)
            pe.wait_ge(s_wide, 1)
            pe.matmul(ps[3][:, 0:D], bwide[:], raw["s1t"][:], start=True, stop=True).then_inc(s_prod, 1)
            pe.matmul(ps[3][:, D:2 * D], bwide[:], raw["n1t"][:], start=True, stop=True).then_inc(s_prod, 1)

        @block.vector
        def _(dve):
            c = Steps(dve, s_dve)
            dve.memset(zeros[:], 0.0).then_inc(s_zero, 1)
            for k, v in enumerate((EPS_LN, 1.0, 0.5, 0.0)):
                c.do(dve.memset(consts[:, k:k + 1], v))
            c.do(dve.memset(ones_row[:], 1.0))

            def indices(W, NS, SM, V, A, T1, RK, T2, dwin, swin, mi, mf, n, a0, r0, in_tail):
                def m(view, f):
                    return view[:, :, f, :]

                def s3(t, lo, hi):
                    return t[:, :, lo:hi].rearrange("p g c -> p c g")

                c.step(dve.tensor_copy(W[:], dwin[:]))
                c.do(dve.tensor_tensor(NS[:], W[:, :, 0:n + 1], W[:, :, 1:n + 2], ALU.not_equal))
                c.do(dve.tensor_tensor(SM[:], W[:, :, 0:n + 1], W[:, :, 1:n + 2], ALU.is_equal))
                c.step(dve.tensor_scalar(V[:], W[:, :, 1:n + 1], 0.0, None, ALU.is_ge))
                for g in range(G):
                    if in_tail:
                        c.do(dve.tensor_tensor_scan(A[:, g, :], SM[:, g, 0:n], V[:, g, :], a0[:, g:g + 1], ALU.min, ALU.mult))
                    else:
                        c.do(dve.tensor_tensor_scan(A[:, g, :], NS[:, g, 0:n], V[:, g, :], 0.0, ALU.max, ALU.mult))
                c.settle()
                c.step(dve.tensor_tensor(T1[:], SM[:, :, 0:n], A[:], ALU.mult))
                c.do(dve.tensor_copy(m(mf, CONT), s3(T1, 0, n)))
                for g in range(G):
                    c.do(dve.tensor_tensor_scan(RK[:, g, :], T1[:, g, :], T1[:, g, :], r0[:, g:g + 1] if in_tail else 0.0,
                                                ALU.mult, ALU.add))
                c.settle()
                c.step(dve.tensor_scalar(T2[:], RK[:], 1.0, None, ALU.add))
                c.step(dve.reciprocal(m(mf, RDEG), s3(T2, 0, n)))
                c.do(dve.tensor_tensor(m(mi, DST), s3(W, 1, n + 1), s3(A, 0, n), ALU.mult))
                c.step(dve.tensor_copy(T2[:], swin[:]))
                c.do(dve.tensor_tensor(m(mi, SRC), s3(T2, 0, n), s3(A, 0, n), ALU.mult))
                c.step(dve.tensor_tensor(T1[:], A[:], NS[:, :, 1:n + 1], ALU.mult))
                c.step(dve.scalar_tensor_tensor(T2[:], W[:, :, 1:n + 1], -float(NP), T1[:], ALU.add, ALU.mult))
                c.do(dve.tensor_scalar(m(mi, OUT), s3(T2, 0, n), float(NP), None, ALU.add))

            dve.wait_ge(s_win, 48)
            indices(W, NS, SM, V, A, T1, RK, T2, dwin, swin, msb, msf, C, 0.0, 0.0, False)
            c.settle()
            c.step(dve.tensor_copy(carry[:, 0, :], A[:, :, C - 1]))
            dve.tensor_copy(carry[:, 1, :], RK[:, :, C - 1]).then_inc(s_meta, 1)
            c.step(dve.tensor_tensor(T1[:], V[:], A[:], ALU.subtract))
            c.step(dve.tensor_reduce(lanes[:, 0, :], T1[:], AX, ALU.add))
            c.do(dve.tensor_reduce(lead[:, 0:1], lanes[:, 0, :], AX, ALU.max))
            c.step(dve.tensor_scalar(lanes[:, 1, :], lanes[:, 0, :], float(C), float(C), ALU.is_ge, ALU.mult))
            dve.tensor_reduce(lead[:, 1:2], lanes[:, 1, :], AX, ALU.add).then_inc(s_lead, 1)
            dve.wait_ge(s_red, 2)
            c.step(dve.tensor_tensor(lead[:, 0:1], allr[:, 0:1], allr[:, 1:2], ALU.add))
            c.step(dve.tensor_scalar(tl[:], lead[:, 0:1], 1.0 / S, 1.01, ALU.mult, ALU.add))
            dve.tensor_scalar(tail[:], tl[:], 1.0, float(TAIL_MAX), ALU.max, ALU.min).then_inc(s_tail, 1)
            dve.wait_ge(s_tail, 1)
            k_tail = dve.value_load(tail[0:1, 0:1], min_val=1, max_val=TAIL_MAX + 1)
            c.restart()
            dve.sem_inc(s_tmeta, CREDIT)
            with dve.Fori(0, k_tail) as k:
                dve.wait_ge(s_twin, k * 32 + 32)
                dve.wait_ge(s_tout, k * 48 + CREDIT)
                indices(Wt, NSt, SMt, Vt, At, T1t, RKt, T2t, dwt, swt, mst, mstf, S, carry[:, 0, :], carry[:, 1, :], True)
                c.settle()
                c.step(dve.tensor_copy(carry[:, 0, :], At[:, :, S - 1]))
                c.step(dve.tensor_copy(carry[:, 1, :], RKt[:, :, S - 1]))
                c.restart()
                dve.sem_inc(s_tmeta, 1)
            dve.wait_ge(s_w, 16 * 22)
            c.step(dve.tensor_copy(bwide[:], bcol[:, 0:1].to_broadcast([P, P])))
            dve.sem_inc(s_wide, 1)
            dve.wait_ge(s_prod, 5)
            dve.wait_ge(s_pool, 2)
            c.step(dve.scalar_tensor_tensor(tmp[:], ps[0][:, 0:D], 0.5, raw["s0t"][:], ALU.mult, ALU.add))
            c.do(dve.scalar_tensor_tensor(w["g0"][:], ident[:], 2.0, tmp[:], ALU.mult, ALU.add))
            c.do(dve.scalar_tensor_tensor(w["g1"][:], ps[1][:, 0:D], 0.5, raw["n0t"][:], ALU.mult, ALU.add))
            c.do(dve.tensor_scalar(w["g2"][:], ps[2][:, 0:D], 0.5, None, ALU.mult))
            c.do(dve.tensor_scalar(w["g"][:], ps[3][:, D:2 * D], 0.5, None, ALU.mult))
            c.step(dve.tensor_tensor(brow1[:], brow1[:], ps[3][:, 0:D], ALU.add))
            c.step(dve.scalar_tensor_tensor(w["c"][:], brow1[:], 0.5, brow0[:], ALU.mult, ALU.add))


def load_meta(sp, mt, meta, b, u, scattered, meta_in, s_hold):
    if not (isinstance(b, int) and b == 0):
        held(sp, scattered[u], b * (16 * G), s_hold)
    for part, (lo, hi) in zip(meta, PARTS):
        sp.dma_start(mt[u][:, lo:hi, :].rearrange("p f g -> p (f g)"),
                     part[bass.ds(b * S + u, 1)].rearrange("a p f -> p (a f)")).then_inc(meta_in[u], 16)


def gather_rows(pool, table, mt, field, to, gathered):
    for g in range(G):
        pool.indirect_dma_start(out=to[:, g, :], out_offset=None, in_=table,
                                in_offset=bass.IndirectOffsetOnAxis(ap=mt[:, field, g:g + 1], axis=0),
                                bounds_check=N - 1, oob_is_err=False).then_inc(gathered, 16)


def scatter_rows(pool, table, mt, rows, scattered):
    for g in range(G):
        pool.indirect_dma_start(out=table, out_offset=bass.IndirectOffsetOnAxis(ap=mt[:, OUT, g:g + 1], axis=0),
                                in_=rows[:, g, :], in_offset=None,
                                bounds_check=N - 1, oob_is_err=False).then_inc(scattered, 16)


def mean_pass(nc, meta, tail, source, table, zeros, tables):
    with ExitStack() as ctx:
        sems = []
        ctx.callback(nc.all_engine_barrier)
        ctx.callback(nc.clear_and_free_semaphores, sems)

        def sb(n, shape, dt=F32):
            return ctx.enter_context(nc.sbuf_tensor("mean_" + n, shape, dt))

        def sem(n):
            sems.append(nc.alloc_semaphore("mean_" + n))
            return sems[-1]

        mt = [sb(f"mt{u}", [P, FIELDS, G], I32) for u in range(S)]
        mf = [t[:].bitcast(F32) for t in mt]
        msg, run, row = ([sb(f"{n}{u}", [P, G, D]) for u in range(S)] for n in ("msg", "run", "row"))
        meta_in, gathered, scattered = ([sem(f"{n}{u}") for u in range(S)] for n in ("meta_in", "gathered", "scattered"))
        s_sum, s_row, s_init, s_hold, s_zeroed = sem("sum"), sem("row"), sem("init"), sem("hold"), sem("zeroed")
        block = ctx.enter_context(nc.Block())

        @block.sync
        def _(sp):
            n = blocks_of(sp, tail)
            pipeline(n, S, sp, [(0, lambda b, u: load_meta(sp, mt, meta, b, u, scattered, meta_in, s_hold))])
            for u in range(S):
                held(sp, scattered[u], n * (16 * G), s_hold)

        @block.gpsimd
        def _(pool):
            def gather(b, u):
                held(pool, meta_in[u], b * 48 + 48, s_hold)
                gather_rows(pool, source, mt[u], SRC, msg[u], gathered[u])

            def scatter(b, u):
                held(pool, s_row, done(b * S + u), s_hold)
                scatter_rows(pool, table, mt[u], row[u], scattered[u])

            pipeline(blocks_of(pool, tail), S, pool, [(0, gather), (3, scatter)])

        @block.vector
        def _(dve):
            n = blocks_of(dve, tail)
            dve.memset(run[S - 1][:], 0.0).then_inc(s_sum, CREDIT)
            with dve.Fori(0, n) as b:
                for u in range(S):
                    dve.wait_ge(gathered[u], b * (16 * G) + 16 * G)
                    dve.wait_ge(s_row, freed(b * S + u, S))
                    dve.wait_ge(s_sum, done(b * S + u - 1))
                    for g in range(G):
                        ins = dve.scalar_tensor_tensor(run[u][:, g, :], run[u - 1][:, g, :], mf[u][:, CONT, g:g + 1],
                                                       msg[u][:, g, :], ALU.mult, ALU.add)
                    ins.then_inc(s_sum, 1)

        @block.scalar
        def _(act):
            n = blocks_of(act, tail)
            act.sem_inc(s_row, CREDIT)
            count = sum(clear_table(act, t, zeros, s_zeroed) for t in tables)
            with act.Fori(0, n) as b:
                for u in range(S):
                    act.wait_ge(s_sum, done(b * S + u))
                    act.wait_ge(meta_in[u], b * 48 + 48)
                    for g in range(G):
                        ins = act.activation(row[u][:, g, :], run[u][:, g, :], ACT.Copy, scale=mf[u][:, RDEG, g:g + 1])
                    ins.then_inc(s_row, 1)
            act.wait_ge(s_zeroed, 16 * count)


def second_mean_pass(nc, meta, tail, x, t_mean, t_part, t_z, ident, w):
    with ExitStack() as ctx:
        sems = []
        ctx.callback(nc.all_engine_barrier)
        ctx.callback(nc.clear_and_free_semaphores, sems)

        def sb(n, shape, dt=F32):
            return ctx.enter_context(nc.sbuf_tensor("two_" + n, shape, dt))

        def sem(n):
            sems.append(nc.alloc_semaphore("two_" + n))
            return sems[-1]

        H = range(WITH)
        mt = [sb(f"mt{u}", [P, FIELDS, G], I32) for u in range(S)]
        mf = [t[:].bitcast(F32) for t in mt]
        msg, run, row, zr = ([sb(f"{n}{u}", [P, G, D]) for u in range(S)] for n in ("msg", "run", "row", "zr"))
        rt = sb("rt", [P, G * P])
        xi, mi, vo = ([[sb(f"{n}{u}{h}", [P, NB, D]) for h in H] for u in range(S)] for n in ("xi", "mi", "vo"))
        xt, mtr = ([sb(f"{n}{h}", [P, BN]) for h in H] for n in ("xt", "mtr"))
        p_x, p_m, p_v = ([ctx.enter_context(nc.psum_tensor(f"two_{n}{h}", [P, BN], F32)) for h in H] for n in "xmv")
        p_r, p_z = (ctx.enter_context(nc.psum_tensor(f"two_{n}", [P, BN], F32)) for n in ("pr", "pz"))
        meta_in, gathered, scattered, loaded, stored = (
            [sem(f"{n}{u}") for u in range(S)] for n in ("meta_in", "gathered", "scattered", "loaded", "stored"))
        s_trx, s_xt, s_mt, s_vm, s_v = ([sem(f"{n}{h}") for h in H] for n in ("trx", "xt", "mt", "vm", "v"))
        s_sum, s_row, s_hold, s_trr, s_rt, s_zm, s_z = (sem(n) for n in ("sum", "row", "hold", "trr", "rt", "zm", "z"))
        block = ctx.enter_context(nc.Block())

        def step(b, u):
            return b * S + u

        def batch(b, u, h):
            return (b * S + u) * WITH + h

        @block.sync
        def _(sp):
            n = blocks_of(sp, tail)

            def load_column(b, u):
                load_meta(sp, mt, meta, b, u, scattered, meta_in, s_hold)

            def load_nodes(b, u):
                for h in H:
                    held(sp, s_trx[h], freed(step(b, u), S), s_hold)
                for h in H:
                    sp.dma_start(flat(xi[u][h]), node_view(x, batch(b, u, h))).then_inc(loaded[u], 16)
                    sp.dma_start(flat(mi[u][h]), node_view(t_mean, batch(b, u, h))).then_inc(loaded[u], 16)

            def store_nodes(b, u):
                for h in H:
                    held(sp, s_v[h], done(step(b, u)), s_hold)
                    sp.dma_start(node_view(t_part, batch(b, u, h)), flat(vo[u][h])).then_inc(stored[u], 16)

            pipeline(MAIN, S, sp, [(0, load_column), (0, load_nodes), (4, store_nodes)])
            with sp.Fori(MAIN, n) as b:
                for u in range(S):
                    load_column(b, u)
            for u in range(S):
                held(sp, scattered[u], n * (16 * G), s_hold)
                held(sp, stored[u], MAIN * (16 * WITH), s_hold)

        @block.gpsimd
        def _(pool):
            def gather(b, u):
                held(pool, meta_in[u], b * 48 + 48, s_hold)
                gather_rows(pool, t_mean, mt[u], SRC, msg[u], gathered[u])

            def scatter(b, u):
                held(pool, s_z, done(step(b, u)), s_hold)
                scatter_rows(pool, t_z, mt[u], zr[u], scattered[u])

            pipeline(blocks_of(pool, tail), S, pool, [(0, gather), (3, scatter)])

        @block.tensor
        def _(pe):
            for s in (*s_trx, *s_vm, s_trr, s_zm):
                pe.sem_inc(s, CREDIT)

            def transpose_nodes(b, u):
                pe.wait_ge(loaded[u], b * (32 * WITH) + 32 * WITH)
                for h in H:
                    pe.wait_ge(s_xt[h], freed(step(b, u), 1))
                    pe.wait_ge(s_mt[h], freed(step(b, u), 1))
                    for src, bank in ((xi, p_x), (mi, p_m)):
                        for j in range(NB):
                            ins = pe.transpose(bank[h][:, j * P:(j + 1) * P], src[u][h][:, j, :], ident[:])
                    ins.then_inc(s_trx[h], 1)

            def node_products(b, u):
                for h in H:
                    pe.wait_ge(s_xt[h], done(step(b, u)))
                    pe.wait_ge(s_mt[h], done(step(b, u)))
                    pe.wait_ge(s_v[h], freed(step(b, u), 1))
                    for j in range(NB):
                        pe.matmul(p_v[h][:, j * D:(j + 1) * D], xt[h][:, j * P:(j + 1) * P], w["g0"][:], start=True, stop=False)
                        ins = pe.matmul(p_v[h][:, j * D:(j + 1) * D], mtr[h][:, j * P:(j + 1) * P], w["g1"][:],
                                        start=False, stop=True)
                    ins.then_inc(s_vm[h], 1)

            def transpose_rows(b, u):
                pe.wait_ge(s_row, done(step(b, u)))
                pe.wait_ge(s_rt, freed(step(b, u), 1))
                for g in range(G):
                    ins = pe.transpose(p_r[:, g * P:(g + 1) * P], row[u][:, g, :], ident[:])
                ins.then_inc(s_trr, 1)

            def row_products(b, u):
                pe.wait_ge(s_rt, done(step(b, u)))
                pe.wait_ge(s_z, freed(step(b, u), 1))
                for g in range(G):
                    ins = pe.matmul(p_z[:, g * D:(g + 1) * D], rt[:, g * P:(g + 1) * P], w["g2"][:], start=True, stop=True)
                ins.then_inc(s_zm, 1)

            pipeline(blocks_of(pe, tail), S, pe,
                     [(0, transpose_nodes, True), (1, transpose_rows), (0, node_products, True), (1, row_products)], MAIN)

        @block.scalar
        def _(act):
            for s in (*s_xt, s_row, s_rt):
                act.sem_inc(s, CREDIT)

            def copy_nodes(b, u):
                for h in H:
                    act.wait_ge(s_trx[h], done(step(b, u)))
                    act.wait_ge(s_vm[h], freed(step(b, u), 1))
                    act.activation(xt[h][:], p_x[h][:], ACT.Copy).then_inc(s_xt[h], 1)

            def copy_rows(b, u):
                act.wait_ge(s_trr, done(step(b, u)))
                act.wait_ge(s_zm, freed(step(b, u), 1))
                act.activation(rt[:], p_r[:], ACT.Copy).then_inc(s_rt, 1)

            def scale(b, u):
                act.wait_ge(s_sum, done(step(b, u)))
                act.wait_ge(s_trr, freed(step(b, u), S))
                act.wait_ge(meta_in[u], b * 48 + 48)
                for g in range(G):
                    ins = act.activation(row[u][:, g, :], run[u][:, g, :], ACT.Copy, scale=mf[u][:, RDEG, g:g + 1])
                ins.then_inc(s_row, 1)

            pipeline(blocks_of(act, tail), S, act, [(0, copy_nodes, True), (1, copy_rows), (0, scale)], MAIN)

        @block.vector
        def _(dve):
            dve.memset(run[S - 1][:], 0.0).then_inc(s_sum, CREDIT)
            for s in (*s_mt, *s_v, s_z):
                dve.sem_inc(s, CREDIT)

            def copy_nodes(b, u):
                for h in H:
                    dve.wait_ge(s_trx[h], done(step(b, u)))
                    dve.wait_ge(s_vm[h], freed(step(b, u), 1))
                    dve.tensor_copy(mtr[h][:], p_m[h][:]).then_inc(s_mt[h], 1)

            def sums(b, u):
                dve.wait_ge(gathered[u], b * (16 * G) + 16 * G)
                dve.wait_ge(s_row, freed(step(b, u), S))
                dve.wait_ge(s_sum, done(step(b, u) - 1))
                for g in range(G):
                    ins = dve.scalar_tensor_tensor(run[u][:, g, :], run[u - 1][:, g, :], mf[u][:, CONT, g:g + 1],
                                                   msg[u][:, g, :], ALU.mult, ALU.add)
                ins.then_inc(s_sum, 1)

            def node_values(b, u):
                dve.wait_ge(stored[u], b * (16 * WITH))
                for h in H:
                    dve.wait_ge(s_vm[h], done(step(b, u)))
                    dve.tensor_tensor(vo[u][h][:], p_v[h][:].rearrange("p (r d) -> p r d", r=NB), over_rows(w["c"][:], NB),
                                      ALU.add).then_inc(s_v[h], 1)

            def row_values(b, u):
                dve.wait_ge(s_zm, done(step(b, u)))
                dve.wait_ge(scattered[u], b * (16 * G))
                dve.tensor_tensor(zr[u][:], p_z[:].rearrange("p (g d) -> p g d", g=G), over_rows(w["g"][:], G),
                                  ALU.add).then_inc(s_z, 1)

            pipeline(blocks_of(dve, tail), S, dve,
                     [(0, copy_nodes, True), (0, sums), (0, node_values, True), (1, row_values)], MAIN)


def rstd_on_pool(pool, c, mv, half_neg, rs, tmp):
    c.do(pool.tensor_scalar(tmp[:, 0, :], mv[:, :, 1], EPS_LN, None, ALU.add))
    c.step(pool.tensor_scalar(tmp[:, 1, :], mv[:, :, 0], -1.0, None, ALU.mult))
    c.step(pool.tensor_tensor(rs[:, 0, :], tmp[:, 0, :], half_neg[:], ALU.pow))
    c.step(pool.tensor_tensor(rs[:, 1, :], tmp[:, 1, :], rs[:, 0, :], ALU.mult))


def node_view(table, t, width=D):
    return table[bass.ds(t * BN, BN)].rearrange("(p r) d -> p (r d)", p=P)


def doubled_scale(pool, c, half_neg, rs, tmp):
    c.step(pool.tensor_tensor(tmp[:, 2, :], rs[:, 0, :], rs[:, 0, :], ALU.mult))
    c.step(pool.tensor_scalar(tmp[:, 2, :], tmp[:, 2, :], -EPS_LN, 1.0 + EPS_LN / 4, ALU.mult, ALU.add))
    c.step(pool.tensor_tensor(rs[:, 2, :], tmp[:, 2, :], half_neg[:], ALU.pow))


def sage_nodes(nc, t_part, t_z, x1, x2):
    with ExitStack() as ctx:
        sems = []
        ctx.callback(nc.all_engine_barrier)
        ctx.callback(nc.clear_and_free_semaphores, sems)

        def sb(n, shape, dt=F32):
            return ctx.enter_context(nc.sbuf_tensor("sage_" + n, shape, dt))

        def sem(n):
            sems.append(nc.alloc_semaphore("sage_" + n))
            return sems[-1]

        part, z, v, o1, o2 = ([sb(f"{n}{u}", [P, NB, D]) for u in range(SN)] for n in ("part", "z", "v", "o1", "o2"))
        st = [sb(f"st{u}", [P, NB, 6]) for u in range(SN)]
        mv = [sb(f"mv{u}", [P, NB, 2]) for u in range(SN)]
        rs, tmp = ([sb(f"{n}{u}", [P, 3, NB]) for u in range(SN)] for n in ("rs", "tmp"))
        half_neg = sb("half_neg", [P, NB])
        loaded, stored = ([sem(f"{n}{u}") for u in range(SN)] for n in ("loaded", "stored"))
        s_v, s_st, s_rs, s_o1, s_o2 = (sem(k) for k in ("v", "st", "rs", "o1", "o2"))
        s_dve, s_pool, s_hold = sem("dve"), sem("pool"), sem("hold")
        IT = BATCHES // SN
        block = ctx.enter_context(nc.Block())

        @block.sync
        def _(sp):
            def load(i, u):
                t = i * SN + u
                held(sp, s_v, freed(t, SN), s_hold)
                sp.dma_start(flat(part[u]), node_view(t_part, t)).then_inc(loaded[u], 16)
                sp.dma_start(flat(z[u]), node_view(t_z, t)).then_inc(loaded[u], 16)

            def store(i, u):
                t = i * SN + u
                held(sp, s_o2, done(t), s_hold)
                sp.dma_start(node_view(x1, t), flat(o1[u])).then_inc(stored[u], 16)
                sp.dma_start(node_view(x2, t), flat(o2[u])).then_inc(stored[u], 16)

            pipeline(IT, SN, sp, [(0, load), (3, store)])
            for u in range(SN):
                held(sp, stored[u], 32 * IT, s_hold)

        @block.scalar
        def _(act):
            act.preload_act_table_set("natural_log_exp_and_others")
            act.sem_inc(s_o1, CREDIT)

            def norm(i, u):
                act.wait_ge(s_rs, done(i * SN + u))
                act.wait_ge(stored[u], i * 32)
                for j in range(NB):
                    ins = act.activation(o1[u][:, j, :], v[u][:, j, :], ACT.Identity, bias=rs[u][:, 1, j:j + 1], scale=rs[u][:, 0, j:j + 1])
                ins.then_inc(s_o1, 1)

            pipeline(IT, SN, act, [(0, norm)])

        @block.vector
        def _(dve):
            c = Steps(dve, s_dve)
            for s in (s_v, s_st, s_o2):
                dve.sem_inc(s, CREDIT)

            def values(i, u):
                t = i * SN + u
                dve.wait_ge(loaded[u], i * 32 + 32)
                dve.wait_ge(s_o1, freed(t, SN))
                dve.tensor_tensor(v[u][:], part[u][:], z[u][:], ALU.add).then_inc(s_v, 1)
                dve.wait_ge(s_v, done(t))
                for j in range(NB):
                    c.do(dve.bn_stats(out=st[u][:, j, :], in_=v[u][:, j, :]))
                c.settle()
                for j in range(NB):
                    ins = dve.bn_aggr(out=mv[u][:, j, :], in_=st[u][:, j, :])
                ins.then_inc(s_st, 1)
                c.restart()

            def double(i, u):
                t = i * SN + u
                dve.wait_ge(s_o1, done(t))
                dve.wait_ge(stored[u], i * 32)
                dve.tensor_tensor(o2[u][:], o1[u][:], lanes_of(rs[u][:, 2, :], NB), ALU.mult).then_inc(s_o2, 1)

            pipeline(IT, SN, dve, [(0, values), (2, double)])

        @block.gpsimd
        def _(pool):
            c = Steps(pool, s_pool)
            pool.sem_inc(s_rs, CREDIT)
            c.step(pool.memset(half_neg[:], -0.5))
            c.restart()

            def scales(i, u):
                t = i * SN + u
                held(pool, s_st, done(t), s_hold)
                held(pool, s_o2, freed(t, SN), s_hold)
                rstd_on_pool(pool, c, mv[u], half_neg, rs[u], tmp[u])
                doubled_scale(pool, c, half_neg, rs[u], tmp[u])
                c.restart()
                pool.sem_inc(s_rs, 1)

            pipeline(IT, SN, pool, [(0, scales)])


def mobius_pass(nc, meta, tail, x1, x2, consts):
    with ExitStack() as ctx:
        sems = []
        ctx.callback(nc.all_engine_barrier)
        ctx.callback(nc.clear_and_free_semaphores, sems)

        def sb(n, shape, dt=F32):
            return ctx.enter_context(nc.sbuf_tensor("mob_" + n, shape, dt))

        def sem(n):
            sems.append(nc.alloc_semaphore("mob_" + n))
            return sems[-1]

        mt = [sb(f"mt{u}", [P, FIELDS, G], I32) for u in range(S)]
        mf = [t[:].bitcast(F32) for t in mt]
        xs, xd, msg, run, v, row = ([sb(f"{n}{u}", [P, G, D]) for u in range(S)] for n in ("xs", "xd", "msg", "run", "v", "row"))
        prod_m, prod_s, prod_v = (sb(f"prod_{k}", [P, G, D]) for k in "msv")
        junk = sb("junk", [P, 4, G, D])
        nrm = [sb(f"nrm{u}", [P, 4, G]) for u in range(S)]
        q = [sb(f"q{u}", [P, 22, G]) for u in range(S)]
        sc = sb("sc", [P, 10, G])
        lg = [sb(f"lg{u}", [P, 5, G]) for u in range(S)]
        st = [sb(f"st{u}", [P, G, 6]) for u in range(S)]
        mv = [sb(f"mv{u}", [P, G, 2]) for u in range(S)]
        rs = [sb(f"rs{u}", [P, 3, G]) for u in range(S)]
        eps_ln, one = consts[:, 0:1], consts[:, 1:2]

        meta_in, gathered, scattered = ([sem(f"{n}{u}") for u in range(S)] for n in ("meta_in", "gathered", "scattered"))
        s_sq, s_ab, s_part, s_msg, s_msq, s_run, s_rsq, s_log, s_arg, s_exp, s_cd, s_vc, s_vpart, s_st, s_rs, s_nb, s_row = (
            sem(k) for k in ("sq", "ab", "part", "msg", "msq", "run", "rsq", "log", "arg", "exp", "cd", "vc", "vpart", "st", "rs",
                             "nb", "row"))
        s_dve, s_act, s_hold = sem("dve"), sem("act"), sem("hold")
        block = ctx.enter_context(nc.Block())

        @block.sync
        def _(sp):
            n = blocks_of(sp, tail)
            pipeline(n, S, sp, [(0, lambda b, u: load_meta(sp, mt, meta, b, u, scattered, meta_in, s_hold))])
            for u in range(S):
                held(sp, scattered[u], n * (16 * G), s_hold)

        @block.gpsimd
        def _(pool):
            def gather(b, u):
                held(pool, meta_in[u], b * 48 + 48, s_hold)
                gather_rows(pool, x1, mt[u], SRC, xs[u], gathered[u])
                gather_rows(pool, x1, mt[u], DST, xd[u], gathered[u])

            def scatter(b, u):
                held(pool, s_row, done(b * S + u), s_hold)
                scatter_rows(pool, x2, mt[u], row[u], scattered[u])

            pipeline(blocks_of(pool, tail), S, pool, [(0, gather), (4, scatter)])

        @block.scalar
        def _(act):
            act.preload_act_table_set("natural_log_exp_and_others")
            c = Steps(act, s_act)
            for s in (s_sq, s_part, s_msq, s_rsq, s_log, s_exp, s_vpart, s_rs, s_row):
                act.sem_inc(s, CREDIT)

            def square(k, src, u):
                for g in range(G):
                    ins = act.activation(junk[:, k, g, :], src[u][:, g, :], ACT.Square, accum_out=nrm[u][:, k, g:g + 1])
                return ins

            def squares(b, u):
                t = b * S + u
                act.wait_ge(gathered[u], b * (32 * G) + 32 * G)
                act.wait_ge(s_nb, freed(t, S))
                act.wait_ge(s_sq, done(t - 1))
                square(0, xs, u)
                square(1, xd, u).then_inc(s_sq, 1)

            def message_part(b, u):
                act.wait_ge(s_ab, done(b * S + u))
                for g in range(G):
                    ins = act.activation(msg[u][:, g, :], xd[u][:, g, :], ACT.Copy, scale=q[u][:, 7, g:g + 1])
                ins.then_inc(s_part, 1)

            def message_square(b, u):
                act.wait_ge(s_msg, done(b * S + u))
                act.wait_ge(s_msq, done(b * S + u - 1))
                square(2, msg, u).then_inc(s_msq, 1)

            def run_square(b, u):
                act.wait_ge(s_run, done(b * S + u))
                act.wait_ge(s_rsq, done(b * S + u - 1))
                square(3, run, u).then_inc(s_rsq, 1)

            def logs(b, u):
                act.wait_ge(s_cd, done(b * S + u))
                c.step(act.activation(lg[u][:, 1, :], lg[u][:, 0, :], ACT.Ln))
                c.step(act.activation(lg[u][:, 2, :], lg[u][:, 1, :], ACT.Exp, scale=0.5))
                c.do(act.activation(lg[u][:, 4, :], lg[u][:, 0, :], ACT.Ln, bias=one, scale=-1.0))
                act.activation(lg[u][:, 3, :], lg[u][:, 2, :], ACT.Ln, bias=one).then_inc(s_log, 1)
                c.restart()

            def exps(b, u):
                act.wait_ge(s_arg, done(b * S + u))
                act.activation(q[u][:, 10, :], q[u][:, 9, :], ACT.Exp).then_inc(s_exp, 1)

            def value_part(b, u):
                act.wait_ge(s_vc, done(b * S + u))
                for g in range(G):
                    ins = act.activation(v[u][:, g, :], run[u][:, g, :], ACT.Copy, scale=q[u][:, 21, g:g + 1])
                ins.then_inc(s_vpart, 1)

            def rstd(b, u):
                act.wait_ge(s_st, done(b * S + u))
                c.step(act.activation(rs[u][:, 0, :], mv[u][:, :, 1], ACT.Ln, bias=eps_ln))
                act.activation(rs[u][:, 1, :], rs[u][:, 0, :], ACT.Exp, scale=-0.5).then_inc(s_rs, 1)
                c.restart()

            def norm(b, u):
                act.wait_ge(s_nb, done(b * S + u))
                act.wait_ge(meta_in[u], b * 48 + 48)
                for g in range(G):
                    ins = act.activation(row[u][:, g, :], v[u][:, g, :], ACT.Identity, bias=rs[u][:, 2, g:g + 1], scale=rs[u][:, 1, g:g + 1])
                ins.then_inc(s_row, 1)

            pipeline(blocks_of(act, tail), S, act,
                     [(0, squares), (3, exps), (0, message_part), (3, value_part), (0, message_square), (3, rstd),
                      (1, run_square), (2, logs), (3, norm)])

        @block.vector
        def _(dve):
            c = Steps(dve, s_dve)
            c.do(dve.memset(run[S - 1][:], 0.0))
            c.step(dve.memset(nrm[S - 1][:, 3, :], 0.0))
            c.restart()
            for s in (s_ab, s_msg, s_run, s_cd, s_arg, s_st, s_vc, s_nb):
                dve.sem_inc(s, CREDIT)
            ts, tt, stt = dve.tensor_scalar, dve.tensor_tensor, dve.scalar_tensor_tensor

            def message_factors(b, u):
                dve.wait_ge(gathered[u], b * (32 * G) + 32 * G)
                dve.wait_ge(s_row, freed(b * S + u, S))
                k = q[u]
                c.step(tt(prod_m[:], xs[u][:], xd[u][:], ALU.mult))
                c.step(dve.tensor_reduce(k[:, 0, :], prod_m[:], AX, ALU.add))
                c.do(ts(k[:, 1, :], k[:, 0, :], -2.0, 1.0, ALU.mult, ALU.add))
                dve.wait_ge(s_sq, done(b * S + u))
                c.step(tt(k[:, 2, :], nrm[u][:, 0, :], nrm[u][:, 1, :], ALU.mult))
                c.step(tt(k[:, 2, :], k[:, 2, :], k[:, 1, :], ALU.add))
                c.do(tt(k[:, 3, :], k[:, 1, :], nrm[u][:, 1, :], ALU.add))
                c.step(ts(k[:, 2, :], k[:, 2, :], EPS, None, ALU.max))
                c.step(dve.reciprocal(k[:, 5, :], k[:, 2, :]))
                c.do(tt(k[:, 6, :], k[:, 3, :], k[:, 5, :], ALU.mult))
                stt(k[:, 7, :], nrm[u][:, 0, :], -1.0, k[:, 5, :], ALU.add, ALU.mult).then_inc(s_ab, 1)

            def messages(b, u):
                c.settle()
                dve.wait_ge(s_part, done(b * S + u))
                for g in range(G):
                    ins = stt(msg[u][:, g, :], xs[u][:, g, :], q[u][:, 6, g:g + 1], msg[u][:, g, :], ALU.mult, ALU.add)
                ins.then_inc(s_msg, 1)

            def scan(b, u):
                t = b * S + u
                dve.wait_ge(s_msq, done(t))
                dve.wait_ge(s_run, done(t - 1))
                prev, cont, m2 = run[u - 1], mf[u][:, CONT, :], nrm[u][:, 2, :]
                c.step(tt(prod_s[:], prev[:], msg[u][:], ALU.mult))
                c.do(dve.tensor_reduce(sc[:, 0, :], prod_s[:], AX, ALU.add))
                if not (isinstance(b, int) and b == 0 and u == 0):
                    dve.wait_ge(s_rsq, done(t - 1))
                c.step(tt(sc[:, 1, :], nrm[u - 1][:, 3, :], cont, ALU.mult))
                c.do(ts(sc[:, 6, :], sc[:, 1, :], -1.0, 1.0, ALU.mult, ALU.add))
                c.do(tt(sc[:, 4, :], sc[:, 1, :], m2, ALU.mult))
                c.step(stt(sc[:, 2, :], sc[:, 0, :], 2.0, cont, ALU.mult, ALU.mult))
                c.do(stt(sc[:, 3, :], sc[:, 2, :], 1.0, m2, ALU.add, ALU.add))
                c.step(stt(sc[:, 5, :], sc[:, 2, :], 1.0, sc[:, 4, :], ALU.add, ALU.add))
                c.step(ts(sc[:, 5, :], sc[:, 5, :], EPS, None, ALU.max))
                c.do(tt(sc[:, 3, :], sc[:, 3, :], cont, ALU.mult))
                c.step(dve.reciprocal(sc[:, 7, :], sc[:, 5, :]))
                c.do(tt(sc[:, 9, :], sc[:, 6, :], sc[:, 7, :], ALU.mult))
                c.step(tt(sc[:, 8, :], sc[:, 3, :], sc[:, 7, :], ALU.mult))
                c.step(tt(prod_s[:], prev[:], lanes_of(sc[:, 8, :], G), ALU.mult))
                for g in range(G):
                    ins = stt(run[u][:, g, :], msg[u][:, g, :], sc[:, 9, g:g + 1], prod_s[:, g, :], ALU.mult, ALU.add)
                ins.then_inc(s_run, 1)

            def clip(b, u):
                dve.wait_ge(s_rsq, done(b * S + u))
                ts(lg[u][:, 0, :], nrm[u][:, 3, :], EPS * EPS, ONE_MINUS_SQ, ALU.max, ALU.min).then_inc(s_cd, 1)

            def arguments(b, u):
                dve.wait_ge(s_log, done(b * S + u))
                k = q[u]
                c.step(stt(k[:, 8, :], lg[u][:, 3, :], 2.0, lg[u][:, 4, :], ALU.mult, ALU.subtract))
                tt(k[:, 9, :], k[:, 8, :], mf[u][:, RDEG, :], ALU.mult).then_inc(s_arg, 1)

            def value_factors(b, u):
                k = q[u]
                c.step(tt(prod_v[:], xd[u][:], run[u][:], ALU.mult))
                c.do(dve.tensor_reduce(k[:, 11, :], prod_v[:], AX, ALU.add))
                c.do(dve.reciprocal(k[:, 12, :], lg[u][:, 2, :]))
                dve.wait_ge(s_exp, done(b * S + u))
                c.step(ts(k[:, 13, :], k[:, 10, :], 1.0, None, ALU.add))
                c.step(dve.reciprocal(k[:, 13, :], k[:, 13, :]))
                c.step(stt(k[:, 13, :], k[:, 10, :], -1.0, k[:, 13, :], ALU.add, ALU.mult))
                c.step(tt(k[:, 13, :], k[:, 13, :], k[:, 12, :], ALU.mult))
                c.step(stt(k[:, 13, :], nrm[u][:, 3, :], EPS * EPS, k[:, 13, :], ALU.is_gt, ALU.mult))
                c.do(tt(k[:, 14, :], k[:, 13, :], k[:, 13, :], ALU.mult))
                c.step(tt(k[:, 15, :], k[:, 13, :], k[:, 11, :], ALU.mult))
                c.do(tt(k[:, 14, :], k[:, 14, :], nrm[u][:, 3, :], ALU.mult))
                c.do(ts(k[:, 17, :], nrm[u][:, 1, :], -1.0, 1.0, ALU.mult, ALU.add))
                c.step(ts(k[:, 15, :], k[:, 15, :], 2.0, 1.0, ALU.mult, ALU.add))
                c.do(tt(k[:, 16, :], nrm[u][:, 1, :], k[:, 14, :], ALU.mult))
                c.do(tt(k[:, 18, :], k[:, 15, :], k[:, 14, :], ALU.add))
                c.step(tt(k[:, 17, :], k[:, 17, :], k[:, 13, :], ALU.mult))
                c.step(tt(k[:, 16, :], k[:, 16, :], k[:, 15, :], ALU.add))
                c.step(ts(k[:, 16, :], k[:, 16, :], EPS, None, ALU.max))
                c.step(dve.reciprocal(k[:, 19, :], k[:, 16, :]))
                c.do(tt(k[:, 20, :], k[:, 18, :], k[:, 19, :], ALU.mult))
                tt(k[:, 21, :], k[:, 17, :], k[:, 19, :], ALU.mult).then_inc(s_vc, 1)

            def values(b, u):
                k = q[u]
                c.settle()
                c.step(ts(k[:, 20, :], k[:, 20, :], 1.0, None, ALU.add))
                dve.wait_ge(s_vpart, done(b * S + u))
                for g in range(G):
                    c.do(stt(v[u][:, g, :], xd[u][:, g, :], k[:, 20, g:g + 1], v[u][:, g, :], ALU.mult, ALU.add))
                c.settle()
                for g in range(G):
                    c.do(dve.bn_stats(out=st[u][:, g, :], in_=v[u][:, g, :]))
                c.settle()
                for g in range(G):
                    ins = dve.bn_aggr(out=mv[u][:, g, :], in_=st[u][:, g, :])
                ins.then_inc(s_st, 1)

            def bias(b, u):
                dve.wait_ge(s_rs, done(b * S + u))
                stt(rs[u][:, 2, :], mv[u][:, :, 0], -1.0, rs[u][:, 1, :], ALU.mult, ALU.mult).then_inc(s_nb, 1)
                c.restart()

            pipeline(blocks_of(dve, tail), S, dve,
                     [(3, arguments), (0, message_factors), (3, value_factors), (0, messages), (3, values), (2, clip),
                      (1, scan), (3, bias)])


def schnet_edges(nc, a, x2, t_agg, ident, w, w_f1, col, rows, ones_row, half, one):
    with ExitStack() as ctx:
        sems = []
        ctx.callback(nc.all_engine_barrier)
        ctx.callback(nc.clear_and_free_semaphores, sems)

        def sb(n, shape, dt=F32):
            return ctx.enter_context(nc.sbuf_tensor("se_" + n, shape, dt))

        def sem(n):
            sems.append(nc.alloc_semaphore("se_" + n))
            return sems[-1]

        RG = range(SG)
        ic = [sb(f"ic{u}", [P, 2 * JG], I32) for u in RG]
        wc = [sb(f"wc{u}", [P, JG]) for u in RG]
        ft = [sb(f"ft{u}", [RBF, GE]) for u in RG]
        srow = [sb(f"srow{u}", [P, GE], I32) for u in RG]
        scol = [sb(f"scol{u}", [P, JG]) for u in RG]
        eq = [sb(f"eq{u}", [P, JG, GE]) for u in RG]
        cnt = [sb(f"cnt{u}", [P, JG]) for u in RG]
        idx = [sb(f"idx{u}", [P, JG], I32) for u in RG]
        xg = [sb(f"xg{u}", [P, JG, D]) for u in RG]
        xt = [sb(f"xt{u}", [P, GE]) for u in RG]
        ab = [sb(f"ab{u}", [P, GE]) for u in RG]
        sp_t = [sb(f"sp{u}", [P, GE]) for u in RG]
        wij = [sb(f"wij{u}", [P, JG, D]) for u in RG]
        msg = [sb(f"msg{u}", [P, JG, D]) for u in RG]
        tot = [sb(f"tot{u}", [P, JG, D]) for u in RG]
        earlier = sb("earlier", [P, JG, GE])
        dummy = sb("dummy", [P, JG])
        dummy_i = sb("dummy_i", [P, JG], I32)
        junk = sb("junk", [P, JG, GE])
        p_t, p_z, p_w, p_h = (ctx.enter_context(nc.psum_tensor(f"se_p{k}", [P, GE], F32)) for k in "tzwh")
        p_s = [ctx.enter_context(nc.psum_tensor(f"se_s{k}", [P, GE], F32)) for k in range(2)]

        cols_in = [sem(f"cols_in{u}") for u in RG]
        rest_in = [sem(f"rest_in{u}") for u in RG]
        gathered = [sem(f"gathered{u}") for u in RG]
        added = [sem(f"added{u}") for u in RG]
        s_tr, s_xt, s_h, s_z, s_ln, s_sp, s_w, s_wij, s_msg, s_eq, s_sum, s_tot, s_idx, s_abs = (
            sem(k) for k in ("tr", "xt", "h", "z", "ln", "sp", "w", "wij", "msg", "eq", "sum", "tot", "idx", "abs"))
        s_dve, s_act, s_pool, s_hold, s_tri = sem("dve"), sem("act"), sem("pool"), sem("hold"), sem("tri")
        IT = GROUPS // SG
        block = ctx.enter_context(nc.Block())

        @block.sync
        def _(sp):
            def load(i, u):
                t = i * SG + u
                held(sp, added[u], i * (16 * JG), s_hold)
                held(sp, s_z, freed(t, SG), s_hold)
                held(sp, s_wij, freed(t, SG), s_hold)
                held(sp, s_eq, freed(t, SG), s_hold)
                sp.dma_start(ic[u][:], a["e_idx"][bass.ds(t * P, P)]).then_inc(cols_in[u], 16)
                sp.dma_start(wc[u][:], a["e_w"][bass.ds(t * P, P)]).then_inc(rest_in[u], 16)
                sp.dma_start(ft[u][:], a["attr_t"][:, bass.ds(t * GE, GE)]).then_inc(rest_in[u], 16)
                sp.dma_start(srow[u][:], a["src_row"][bass.ds(t, 1)].to_broadcast([P, GE])).then_inc(rest_in[u], 16)

            pipeline(IT, SG, sp, [(0, load)])
            for u in RG:
                held(sp, added[u], 16 * JG * IT, s_hold)

        @block.gpsimd
        def _(pool):
            c = Steps(pool, s_pool)
            c.step(pool.memset(earlier[:], 1.0))
            for j in range(JG):
                ins = pool.affine_select(out=earlier[:, j, :], in_=earlier[:, j, :], compare_op=ALU.is_gt, fill=0.0,
                                         base=P * j, pattern=[[-1, GE]], channel_multiplier=1)
            ins.then_inc(s_tri, 1)
            pool.iota(dummy_i[:], pattern=[[P, JG]], base=DUMMY, channel_multiplier=1).then_inc(s_tri, 1)

            def gather(i, u):
                held(pool, cols_in[u], i * 16 + 16, s_hold)
                for j in range(JG):
                    pool.indirect_dma_start(out=xg[u][:, j, :], out_offset=None, in_=x2,
                                            in_offset=bass.IndirectOffsetOnAxis(ap=ic[u][:, j:j + 1], axis=0),
                                            bounds_check=N - 1, oob_is_err=False).then_inc(gathered[u], 16)

            def add(i, u):
                held(pool, s_idx, done(i * SG + u), s_hold)
                held(pool, s_tot, done(i * SG + u), s_hold)
                if u > 0:
                    held(pool, added[u - 1], i * (16 * JG) + 16 * JG, s_hold)
                else:
                    held(pool, added[SG - 1], i * (16 * JG), s_hold)
                for j in range(JG):
                    pool.indirect_dma_start(out=t_agg, out_offset=bass.IndirectOffsetOnAxis(ap=idx[u][:, j:j + 1], axis=0),
                                            in_=tot[u][:, j, :], in_offset=None,
                                            bounds_check=AGG_ROWS - 1, oob_is_err=True,
                                            compute_op=ALU.add).then_inc(added[u], 16)

            pipeline(IT, SG, pool, [(0, gather), (3, add)])

        @block.tensor
        def _(pe):
            for s in (s_tr, s_h, s_z, s_w, s_sum):
                pe.sem_inc(s, CREDIT)

            def filters(i, u):
                t = i * SG + u
                pe.wait_ge(rest_in[u], i * 48 + 48)
                pe.wait_ge(s_sp, freed(t, 1))
                pe.wait_ge(s_abs, freed(t, 1))
                pe.matmul(p_z[:], w_f1[:], ft[u][:], start=True, stop=True).then_inc(s_z, 1)
                pe.wait_ge(gathered[u], i * (16 * JG) + 16 * JG)
                pe.wait_ge(s_xt, freed(t, 1))
                for j in range(JG):
                    ins = pe.transpose(p_t[:, j * P:(j + 1) * P], xg[u][:, j, :], ident[:])
                ins.then_inc(s_tr, 1)

            def products(i, u):
                t = i * SG + u
                pe.wait_ge(s_xt, done(t))
                pe.wait_ge(s_msg, freed(t, 1))
                pe.matmul(p_h[:], ones_row[0:1, :], rows[0:1, 0, :], start=True, stop=False, skip_group_check=True)
                for j in range(JG):
                    ins = pe.matmul(p_h[:, j * D:(j + 1) * D], xt[u][:, j * P:(j + 1) * P], w["in2f"][:],
                                    start=False, stop=(j == JG - 1), skip_group_check=True)
                ins.then_inc(s_h, 1)
                pe.wait_ge(s_sp, done(t))
                pe.wait_ge(s_wij, freed(t, 1))
                pe.matmul(p_w[:], ones_row[0:1, :], rows[0:1, 1, :], start=True, stop=False, skip_group_check=True)
                for j in range(JG):
                    ins = pe.matmul(p_w[:, j * D:(j + 1) * D], sp_t[u][:, j * P:(j + 1) * P], w["f2"][:],
                                    start=False, stop=(j == JG - 1), skip_group_check=True)
                ins.then_inc(s_w, 1)

            def sums(i, u):
                t = i * SG + u
                pe.wait_ge(s_eq, done(t))
                pe.wait_ge(s_msg, done(t))
                pe.wait_ge(s_tot, freed(t, 2))
                for j in range(JG):
                    for k in range(JG):
                        ins = pe.matmul(p_s[u % 2][:, j * D:(j + 1) * D], eq[u][:, k, j * P:(j + 1) * P], msg[u][:, k, :],
                                        start=(k == 0), stop=(k == JG - 1))
                ins.then_inc(s_sum, 1)

            pipeline(IT, SG, pe, [(1, products), (2, sums), (0, filters)])

        @block.scalar
        def _(act):
            act.preload_act_table_set("natural_log_exp_and_others")
            c = Steps(act, s_act)
            for s in (s_xt, s_ln, s_wij, s_tot, s_abs):
                act.sem_inc(s, CREDIT)

            def softplus(i, u):
                t = i * SG + u
                act.wait_ge(s_z, done(t))
                act.wait_ge(s_sp, freed(t, SG))
                act.activation(ab[u][:], p_z[:], ACT.Abs, bias=col[:, 0:1]).then_inc(s_abs, 1)
                act.wait_ge(s_abs, done(t))
                c.step(act.activation(ab[u][:], ab[u][:], ACT.Exp, scale=-1.0))
                act.activation(ab[u][:], ab[u][:], ACT.Ln, bias=half, scale=0.5).then_inc(s_ln, 1)
                act.wait_ge(s_tr, done(t))
                act.wait_ge(s_h, freed(t, SG))
                act.activation(xt[u][:], p_t[:], ACT.Copy).then_inc(s_xt, 1)

            def weigh(i, u):
                t = i * SG + u
                act.wait_ge(s_w, done(t))
                act.wait_ge(s_msg, freed(t, SG))
                for j in range(JG):
                    ins = act.activation(wij[u][:, j, :], p_w[:, j * D:(j + 1) * D], ACT.Copy, scale=wc[u][:, j:j + 1])
                ins.then_inc(s_wij, 1)
                c.restart()

            def totals(i, u):
                t = i * SG + u
                act.wait_ge(s_sum, done(t))
                act.wait_ge(added[u], i * (16 * JG))
                act.activation(tot[u][:].rearrange("p j d -> p (j d)"), p_s[u % 2][:], ACT.Copy).then_inc(s_tot, 1)

            pipeline(IT, SG, act, [(1, weigh), (2, totals), (0, softplus)])

        @block.vector
        def _(dve):
            c = Steps(dve, s_dve)
            for s in (s_sp, s_msg, s_eq, s_idx):
                dve.sem_inc(s, CREDIT)
            dve.wait_ge(s_tri, 2)
            c.step(dve.tensor_copy(dummy[:], dummy_i[:]))

            def equal(i, u):
                t = i * SG + u
                dve.wait_ge(rest_in[u], i * 48 + 48)
                dve.wait_ge(cols_in[u], i * 16 + 16)
                dve.wait_ge(s_sum, freed(t, SG))
                c.step(dve.tensor_copy(scol[u][:], ic[u][:, JG:2 * JG]))
                for k in range(JG):
                    ins = dve.tensor_scalar(eq[u][:, k, :], srow[u][:], scol[u][:, k:k + 1], None, ALU.is_equal)
                ins.then_inc(s_eq, 1)

            def softplus_sum(i, u):
                t = i * SG + u
                dve.wait_ge(s_abs, done(t))
                dve.wait_ge(s_w, freed(t, SG))
                c.step(dve.tensor_scalar(sp_t[u][:], p_z[:], col[:, 0:1], 0.0, ALU.add, ALU.max))
                dve.wait_ge(s_ln, done(t))
                dve.tensor_tensor(sp_t[u][:], sp_t[u][:], ab[u][:], ALU.add).then_inc(s_sp, 1)

            def first(i, u):
                t = i * SG + u
                dve.wait_ge(s_eq, done(t))
                dve.wait_ge(added[u], i * (16 * JG))
                for k in range(JG):
                    c.do(dve.tensor_tensor_reduce(out=junk[:, k, :], in0=eq[u][:, k, :], in1=earlier[:, k, :], scale=1.0,
                                                  scalar=0.0, op0=ALU.mult, op1=ALU.add, accum_out=cnt[u][:, k:k + 1]))
                c.settle()
                c.do(dve.tensor_scalar(cnt[u][:], cnt[u][:], 0.5, None, ALU.is_lt))
                c.step(dve.tensor_tensor(scol[u][:], scol[u][:], dummy[:], ALU.subtract))
                c.step(dve.tensor_tensor(scol[u][:], scol[u][:], cnt[u][:], ALU.mult))
                dve.tensor_tensor(idx[u][:], scol[u][:], dummy[:], ALU.add).then_inc(s_idx, 1)

            def messages(i, u):
                t = i * SG + u
                dve.wait_ge(s_h, done(t))
                dve.wait_ge(s_wij, done(t))
                dve.tensor_tensor(msg[u][:].rearrange("p j d -> p (j d)"), p_h[:], wij[u][:].rearrange("p j d -> p (j d)"),
                                  ALU.mult).then_inc(s_msg, 1)
                c.restart()

            c.restart()
            pipeline(IT, SG, dve, [(1, messages), (0, equal), (0, first), (0, softplus_sum)])


def schnet_nodes(nc, x2, t_agg, x3, out, ident, w, col, rows, ones_row, half):
    with ExitStack() as ctx:
        sems = []
        ctx.callback(nc.all_engine_barrier)
        ctx.callback(nc.clear_and_free_semaphores, sems)

        def sb(n, shape, dt=F32):
            return ctx.enter_context(nc.sbuf_tensor("sn_" + n, shape, dt))

        def sem(n):
            sems.append(nc.alloc_semaphore("sn_" + n))
            return sems[-1]

        R4 = range(SN)
        xi = [sb(f"x{u}", [P, NB, D]) for u in R4]
        ag = [sb(f"agg{u}", [P, NB, D]) for u in R4]
        at = [sb(f"at{u}", [P, BN]) for u in R4]
        ab = [sb(f"ab{u}", [P, BN]) for u in R4]
        sp_t = [sb(f"sp{u}", [P, BN]) for u in R4]
        v = [sb(f"v{u}", [P, NB, D]) for u in R4]
        st = [sb(f"st{u}", [P, NB, 6]) for u in R4]
        mv = [sb(f"mv{u}", [P, NB, 2]) for u in R4]
        rs = [sb(f"rs{u}", [P, 3, NB]) for u in R4]
        tmp = [sb(f"tmp{u}", [P, 3, NB]) for u in R4]
        o = [sb(f"o{u}", [P, NB, D]) for u in R4]
        o2 = [sb(f"o2{u}", [P, NB, D]) for u in R4]
        half_neg = sb("half_neg", [P, NB])
        p_t, p_z, p_o = ([ctx.enter_context(nc.psum_tensor(f"sn_p{k}{m}", [P, BN], F32)) for m in range(2)] for k in "tzo")
        loaded = [sem(f"loaded{u}") for u in R4]
        stored = [sem(f"stored{u}") for u in R4]
        s_tr, s_at, s_z, s_abs, s_ln, s_sp, s_mm, s_v, s_st, s_rs, s_o, s_o2 = (
            sem(k) for k in ("tr", "at", "z", "abs", "ln", "sp", "mm", "v", "st", "rs", "o", "o2"))
        s_dve, s_act, s_pool, s_hold = sem("dve"), sem("act"), sem("pool"), sem("hold")
        IT = BATCHES // SN
        block = ctx.enter_context(nc.Block())

        @block.sync
        def _(sp):
            def load(i, u):
                t = i * SN + u
                held(sp, s_tr, freed(t, SN), s_hold)
                held(sp, s_v, freed(t, SN), s_hold)
                sp.dma_start(ag[u][:].rearrange("p r d -> p (r d)"), node_view(t_agg, t)).then_inc(loaded[u], 16)
                sp.dma_start(xi[u][:].rearrange("p r d -> p (r d)"), node_view(x2, t)).then_inc(loaded[u], 16)

            def store(i, u):
                t = i * SN + u
                held(sp, s_o, done(t), s_hold)
                held(sp, s_o2, done(t), s_hold)
                sp.dma_start(node_view(x3, t), o[u][:].rearrange("p r d -> p (r d)")).then_inc(stored[u], 16)
                sp.dma_start(node_view(out, t), o2[u][:].rearrange("p r d -> p (r d)")).then_inc(stored[u], 16)

            pipeline(IT, SN, sp, [(0, load), (4, store)])
            for u in R4:
                held(sp, stored[u], 32 * IT, s_hold)

        @block.tensor
        def _(pe):
            for s in (s_tr, s_z, s_mm):
                pe.sem_inc(s, CREDIT)

            def transposes(i, u):
                t = i * SN + u
                pe.wait_ge(loaded[u], i * 32 + 32)
                pe.wait_ge(s_at, freed(t, 2))
                for j in range(NB):
                    ins = pe.transpose(p_t[u % 2][:, j * P:(j + 1) * P], ag[u][:, j, :], ident[:])
                ins.then_inc(s_tr, 1)

            def hidden(i, u):
                t = i * SN + u
                pe.wait_ge(s_at, done(t))
                pe.wait_ge(s_abs, freed(t, 2))
                pe.wait_ge(s_sp, freed(t, 2))
                pe.matmul(p_z[u % 2][:], w["o1"][:], at[u][:], start=True, stop=True).then_inc(s_z, 1)

            def outputs(i, u):
                t = i * SN + u
                pe.wait_ge(s_sp, done(t))
                pe.wait_ge(s_v, freed(t, 2))
                pe.matmul(p_o[u % 2][:], ones_row[0:1, :], rows[0:1, 2, :], start=True, stop=False, skip_group_check=True)
                for j in range(NB):
                    ins = pe.matmul(p_o[u % 2][:, j * D:(j + 1) * D], sp_t[u][:, j * P:(j + 1) * P], w["o2"][:],
                                    start=False, stop=(j == NB - 1), skip_group_check=True)
                ins.then_inc(s_mm, 1)

            pipeline(IT, SN, pe, [(0, transposes), (1, hidden), (2, outputs)])

        @block.scalar
        def _(act):
            act.preload_act_table_set("natural_log_exp_and_others")
            c = Steps(act, s_act)
            for s in (s_at, s_abs, s_ln, s_o):
                act.sem_inc(s, CREDIT)

            def copy(i, u):
                t = i * SN + u
                act.wait_ge(s_tr, done(t))
                act.wait_ge(s_z, freed(t, SN))
                act.activation(at[u][:], p_t[u % 2][:], ACT.Copy).then_inc(s_at, 1)

            def softplus(i, u):
                t = i * SN + u
                act.wait_ge(s_z, done(t))
                act.wait_ge(s_sp, freed(t, SN))
                act.activation(ab[u][:], p_z[u % 2][:], ACT.Abs, bias=col[:, 1:2]).then_inc(s_abs, 1)
                act.wait_ge(s_abs, done(t))
                c.step(act.activation(ab[u][:], ab[u][:], ACT.Exp, scale=-1.0))
                act.activation(ab[u][:], ab[u][:], ACT.Ln, bias=half, scale=0.5).then_inc(s_ln, 1)
                c.restart()

            def norm(i, u):
                act.wait_ge(s_rs, done(i * SN + u))
                act.wait_ge(stored[u], i * 32)
                act.wait_ge(s_o2, freed(i * SN + u, SN))
                for j in range(NB):
                    ins = act.activation(o[u][:, j, :], v[u][:, j, :], ACT.Identity, bias=rs[u][:, 1, j:j + 1], scale=rs[u][:, 0, j:j + 1])
                ins.then_inc(s_o, 1)

            pipeline(IT, SN, act, [(0, copy), (1, softplus), (3, norm)])

        @block.vector
        def _(dve):
            c = Steps(dve, s_dve)
            for s in (s_sp, s_v, s_st):
                dve.sem_inc(s, CREDIT)

            def softplus_sum(i, u):
                t = i * SN + u
                dve.wait_ge(s_abs, done(t))
                dve.wait_ge(s_mm, freed(t, SN))
                c.step(dve.tensor_scalar(sp_t[u][:], p_z[u % 2][:], col[:, 1:2], 0.0, ALU.add, ALU.max))
                dve.wait_ge(s_ln, done(t))
                dve.tensor_tensor(sp_t[u][:], sp_t[u][:], ab[u][:], ALU.add).then_inc(s_sp, 1)

            def values(i, u):
                t = i * SN + u
                dve.wait_ge(s_mm, done(t))
                dve.wait_ge(s_o, freed(t, SN))
                dve.tensor_tensor(v[u][:].rearrange("p r d -> p (r d)"), p_o[u % 2][:], xi[u][:].rearrange("p r d -> p (r d)"),
                                  ALU.add).then_inc(s_v, 1)
                dve.wait_ge(s_v, done(t))
                for j in range(NB):
                    c.do(dve.bn_stats(out=st[u][:, j, :], in_=v[u][:, j, :]))
                c.settle()
                for j in range(NB):
                    ins = dve.bn_aggr(out=mv[u][:, j, :], in_=st[u][:, j, :])
                ins.then_inc(s_st, 1)
                c.restart()

            pipeline(IT, SN, dve, [(1, softplus_sum), (2, values)])

        @block.gpsimd
        def _(pool):
            c = Steps(pool, s_pool)
            pool.sem_inc(s_rs, CREDIT)
            pool.sem_inc(s_o2, CREDIT)
            c.step(pool.memset(half_neg[:], -0.5))
            c.restart()

            def scales(i, u):
                t = i * SN + u
                held(pool, s_st, done(t), s_hold)
                held(pool, s_o, freed(t, SN), s_hold)
                held(pool, s_o2, freed(t, SN), s_hold)
                rstd_on_pool(pool, c, mv[u], half_neg, rs[u], tmp[u])
                doubled_scale(pool, c, half_neg, rs[u], tmp[u])
                c.restart()
                pool.sem_inc(s_rs, 1)

            def double(i, u):
                t = i * SN + u
                held(pool, s_o, done(t), s_hold)
                held(pool, stored[u], i * 32, s_hold)
                pool.tensor_tensor(o2[u][:], o[u][:], lanes_of(rs[u][:, 2, :], NB), ALU.mult).then_inc(s_o2, 1)

            pipeline(IT, SN, pool, [(3, double), (0, scales)])


def last_pass(nc, meta, tail, x3, out, ident, w, bias3, consts):
    with ExitStack() as ctx:
        sems = []
        ctx.callback(nc.all_engine_barrier)
        ctx.callback(nc.clear_and_free_semaphores, sems)

        def sb(n, shape, dt=F32):
            return ctx.enter_context(nc.sbuf_tensor("last_" + n, shape, dt))

        def sem(n):
            sems.append(nc.alloc_semaphore("last_" + n))
            return sems[-1]

        mt = [sb(f"mt{u}", [P, FIELDS, G], I32) for u in range(S)]
        mf = [t[:].bitcast(F32) for t in mt]
        msg, xd, run, row, v, o = ([sb(f"{n}{u}", [P, G, D]) for u in range(S)] for n in ("msg", "xd", "run", "row", "v", "o"))
        xt, rt = sb("xt", [P, G * P]), sb("rt", [P, G * P])
        st = [sb(f"st{u}", [P, G, 6]) for u in range(S)]
        mv = [sb(f"mv{u}", [P, G, 2]) for u in range(S)]
        rs = [sb(f"rs{u}", [P, 3, G]) for u in range(S)]
        p_x, p_r, p_z = (ctx.enter_context(nc.psum_tensor(f"last_{n}", [P, G * D], F32)) for n in "xrz")
        meta_in, gathered, scattered = ([sem(f"{n}{u}") for u in range(S)] for n in ("meta_in", "gathered", "scattered"))
        s_sum, s_row, s_tr, s_t, s_mm, s_z, s_st, s_rs, s_nb, s_o = (
            sem(n) for n in ("sum", "row", "tr", "t", "mm", "z", "st", "rs", "nb", "o"))
        s_dve, s_act, s_hold = sem("dve"), sem("act"), sem("hold")
        eps_ln = consts[:, 0:1]
        block = ctx.enter_context(nc.Block())

        def step(b, u):
            return b * S + u

        @block.sync
        def _(sp):
            n = blocks_of(sp, tail)
            pipeline(n, S, sp, [(0, lambda b, u: load_meta(sp, mt, meta, b, u, scattered, meta_in, s_hold))])
            for u in range(S):
                held(sp, scattered[u], n * (16 * G), s_hold)

        @block.gpsimd
        def _(pool):
            def gather(b, u):
                held(pool, meta_in[u], b * 48 + 48, s_hold)
                gather_rows(pool, x3, mt[u], SRC, msg[u], gathered[u])
                gather_rows(pool, x3, mt[u], DST, xd[u], gathered[u])

            def scatter(b, u):
                held(pool, s_o, done(step(b, u)), s_hold)
                scatter_rows(pool, out, mt[u], o[u], scattered[u])

            pipeline(blocks_of(pool, tail), S, pool, [(0, gather), (3, scatter)])

        @block.tensor
        def _(pe):
            for s in (s_tr, s_mm):
                pe.sem_inc(s, CREDIT)

            def transposes(b, u):
                pe.wait_ge(gathered[u], b * (32 * G) + 32 * G)
                pe.wait_ge(s_row, done(step(b, u)))
                pe.wait_ge(s_t, freed(step(b, u), 1))
                for src, bank in ((xd, p_x), (row, p_r)):
                    for g in range(G):
                        ins = pe.transpose(bank[:, g * P:(g + 1) * P], src[u][:, g, :], ident[:])
                ins.then_inc(s_tr, 1)

            def products(b, u):
                pe.wait_ge(s_t, done(step(b, u)))
                pe.wait_ge(s_z, freed(step(b, u), 1))
                for g in range(G):
                    pe.matmul(p_z[:, g * D:(g + 1) * D], xt[:, g * P:(g + 1) * P], w["h3"][:], start=True, stop=False)
                    ins = pe.matmul(p_z[:, g * D:(g + 1) * D], rt[:, g * P:(g + 1) * P], w["c3"][:], start=False, stop=True)
                ins.then_inc(s_mm, 1)

            pipeline(blocks_of(pe, tail), S, pe, [(1, transposes), (1, products)])

        @block.scalar
        def _(act):
            act.preload_act_table_set("natural_log_exp_and_others")
            c = Steps(act, s_act)
            for s in (s_row, s_t, s_rs, s_o):
                act.sem_inc(s, CREDIT)

            def copies(b, u):
                act.wait_ge(s_tr, done(step(b, u)))
                act.wait_ge(s_mm, freed(step(b, u), 1))
                act.activation(xt[:], p_x[:], ACT.Copy)
                act.activation(rt[:], p_r[:], ACT.Copy).then_inc(s_t, 1)

            def scale(b, u):
                act.wait_ge(s_sum, done(step(b, u)))
                act.wait_ge(s_tr, freed(step(b, u), S))
                for g in range(G):
                    ins = act.activation(row[u][:, g, :], run[u][:, g, :], ACT.Copy, scale=mf[u][:, RDEG, g:g + 1])
                ins.then_inc(s_row, 1)

            def rstd(b, u):
                act.wait_ge(s_st, done(step(b, u)))
                c.step(act.activation(rs[u][:, 0, :], mv[u][:, :, 1], ACT.Ln, bias=eps_ln))
                act.activation(rs[u][:, 1, :], rs[u][:, 0, :], ACT.Exp, scale=-0.5).then_inc(s_rs, 1)
                c.restart()

            def norm(b, u):
                act.wait_ge(s_nb, done(step(b, u)))
                act.wait_ge(meta_in[u], b * 48 + 48)
                for g in range(G):
                    ins = act.activation(o[u][:, g, :], v[u][:, g, :], ACT.Identity, bias=rs[u][:, 2, g:g + 1], scale=rs[u][:, 1, g:g + 1])
                ins.then_inc(s_o, 1)

            pipeline(blocks_of(act, tail), S, act, [(1, copies), (0, scale), (2, norm), (1, rstd)])

        @block.vector
        def _(dve):
            c = Steps(dve, s_dve)
            dve.memset(run[S - 1][:], 0.0).then_inc(s_sum, CREDIT)
            for s in (s_z, s_st, s_nb):
                dve.sem_inc(s, CREDIT)

            def sums(b, u):
                dve.wait_ge(gathered[u], b * (32 * G) + 32 * G)
                dve.wait_ge(s_row, freed(step(b, u), S))
                dve.wait_ge(s_sum, done(step(b, u) - 1))
                for g in range(G):
                    ins = dve.scalar_tensor_tensor(run[u][:, g, :], run[u - 1][:, g, :], mf[u][:, CONT, g:g + 1],
                                                   msg[u][:, g, :], ALU.mult, ALU.add)
                ins.then_inc(s_sum, 1)

            def values(b, u):
                dve.wait_ge(s_mm, done(step(b, u)))
                dve.wait_ge(s_o, freed(step(b, u), S))
                dve.tensor_tensor(v[u][:], p_z[:].rearrange("p (g d) -> p g d", g=G), over_rows(bias3[:], G),
                                  ALU.add).then_inc(s_z, 1)
                dve.wait_ge(s_z, done(step(b, u)))
                c.step(dve.scalar_tensor_tensor(v[u][:], v[u][:], 0.0, xd[u][:], ALU.max, ALU.add))
                for g in range(G):
                    c.do(dve.bn_stats(out=st[u][:, g, :], in_=v[u][:, g, :]))
                c.settle()
                for g in range(G):
                    ins = dve.bn_aggr(out=mv[u][:, g, :], in_=st[u][:, g, :])
                ins.then_inc(s_st, 1)
                c.restart()

            def bias(b, u):
                dve.wait_ge(s_rs, done(step(b, u)))
                dve.scalar_tensor_tensor(rs[u][:, 2, :], mv[u][:, :, 0], -1.0, rs[u][:, 1, :], ALU.mult,
                                         ALU.mult).then_inc(s_nb, 1)

            pipeline(blocks_of(dve, tail), S, dve, [(2, bias), (0, sums), (1, values)])


def kernel(**inputs):
    import numpy as np
    import concourse.bacc as bacc
    from concourse.bass_utils import run_bass_kernel_spmd

    def t(name):
        return np.ascontiguousarray(np.asarray(inputs[name]).T)

    def arr(name):
        return np.asarray(inputs[name])

    src, dst = arr("src"), arr("dst")
    EG = GROUPS * GE
    src_g = np.full(EG, AGG_ROWS - 1, np.int32)
    src_g[:E] = src
    dst_g = np.zeros(EG, np.int32)
    dst_g[:E] = dst
    w_g = np.zeros(EG, np.float32)
    w_g[:E] = arr("edge_weight")
    attr = np.zeros((RBF, EG), np.float32)
    attr[:, :E] = arr("edge_attr_20").T
    dst_pad = np.full(E_PAD, -1, np.int32)
    dst_pad[0] = -2
    dst_pad[1:E + 1] = dst
    src_pad = np.zeros(E_PAD, np.int32)
    src_pad[:E] = src
    x_pad = np.zeros((NP, D), np.float32)
    x_pad[:N] = arr("x")

    def columns(v):
        return v.reshape(GROUPS, JG, P).transpose(0, 2, 1).reshape(GROUPS * P, JG)

    arrays = {
        "x": x_pad, "dst_pad": dst_pad, "src_pad": src_pad,
        "e_idx": np.concatenate([columns(dst_g), columns(src_g)], axis=1), "e_w": columns(w_g),
        "attr_t": attr, "src_row": src_g.reshape(GROUPS, GE),
        "s0": arr("L0_gnn_W_self0"), "n0": arr("L0_gnn_W_neigh0"),
        "s0t": t("L0_gnn_W_self0"), "n0t": t("L0_gnn_W_neigh0"),
        "s1t": t("L0_gnn_W_self1"), "n1t": t("L0_gnn_W_neigh1"),
        "b_self0": arr("L0_gnn_b_self0"), "b_self1": arr("L0_gnn_b_self1"),
        "w_in2f": t("L2_gnn_W_in2f"), "w_f1": t("L2_gnn_W_f1"), "w_f2": t("L2_gnn_W_f2"),
        "w_o1": t("L2_gnn_W_o1"), "w_o2": t("L2_gnn_W_o2"),
        "w_h3": arr("L3_gnn_W")[0:D], "w_c3": arr("L3_gnn_W")[D:2 * D],
        "b_in2f": arr("L2_gnn_b_in2f"), "b_f1": arr("L2_gnn_b_f1"), "b_f2": arr("L2_gnn_b_f2"),
        "b_o1": arr("L2_gnn_b_o1"), "b_o2": arr("L2_gnn_b_o2"), "b_3": arr("L3_gnn_b"),
    }
    nc = bacc.Bacc("TRN2", target_bir_lowering=False, num_devices=1)
    feeds, aps = {}, {}
    for name, value in arrays.items():
        value = np.ascontiguousarray(value)
        feeds["in_" + name] = value
        aps[name] = nc.dram_tensor("in_" + name, value.shape, mybir.dt.from_np(value.dtype), kind="ExternalInput").ap()
    out = nc.dram_tensor("out_nodes", [NP, D], F32, kind="ExternalOutput").ap()
    gnn_kernel(nc, aps, out)
    result = run_bass_kernel_spmd(nc, [feeds], core_ids=[0])
    return result.results[0]["out_nodes"][:N]
```

```python
from contextlib import ExitStack

import concourse.bass as bass
from concourse import mybir

P = 128
D = 128
N = 100000
E = 50000

G = 4
S = 7
LANES = P * G
C = S * -(-E // (LANES * S))
MAIN = C // S
TAIL_MAX = E // S + 1
FIELDS = 5
SRC, OUT, CONT, RDEG, DST = range(FIELDS)
PARTS = ((SRC, OUT + 1), (CONT, RDEG + 1), (DST, DST + 1))
E_PAD = LANES * C + C + S * (TAIL_MAX + 1)

NB = 4
BN = P * NB
BATCHES = -(-N // BN)
NP = BATCHES * BN
SN = 4
WITH = BATCHES // C
assert WITH * C == BATCHES

JG = 4
GE = P * JG
JH = JG // 2
HE = P * JH
SG = 4
GROUPS = SG * -(-E // (GE * SG))
RBF = 20
DUMMY = NP
AGG_ROWS = NP + GE + 1

EPS_LN = 1e-5
EPS = 1e-7
ONE_MINUS_SQ = float.fromhex("0x1.fffff8p-1")

F32 = mybir.dt.float32
I32 = mybir.dt.int32
ALU = mybir.AluOpType
ACT = mybir.ActivationFunctionType
AX = mybir.AxisListType.X
RED = bass.bass_isa.ReduceOp

CREDIT = 8


def done(t):
    return t + 1 + CREDIT


def freed(t, k):
    return t + 1 + CREDIT - k


def pipeline(blocks, slots, eng, stages, main=None):
    depth = max(stage[0] for stage in stages)
    every = [stage for stage in stages if len(stage) == 2]
    peel = max(1, -(-depth // slots))
    for s in range(peel * slots):
        for d, f, *_ in stages:
            if s >= d:
                f((s - d) // slots, (s - d) % slots)

    def loop(first, last, stages):
        with eng.Fori(first, last) as b:
            for u in range(slots):
                for d, f, *_ in stages:
                    back = (u - d) // slots
                    f(b + back if back else b, (u - d) % slots)

    if main is not None:
        loop(peel, main, stages)
    loop(peel if main is None else main, blocks, every)
    for s in range(depth):
        for d, f in every:
            if s < d:
                back = (s - d) // slots
                f(blocks + back if back else blocks, (s - d) % slots)


def held(eng, sem, value, hold):
    eng.wait_ge(sem, value)
    eng.sem_inc(hold, 1)


class Steps:

    def __init__(self, eng, sem):
        self.eng, self.sem, self.n = eng, sem, 0

    def do(self, ins):
        ins.then_inc(self.sem, 1)
        self.n += 1

    def settle(self, but=0):
        if self.n > but:
            self.eng.wait_ge(self.sem, self.n - but)

    def step(self, ins):
        self.do(ins)
        self.settle()

    def restart(self):
        if self.n:
            self.settle()
            self.eng.sem_clear(self.sem)
            self.n = 0


def lanes_of(v, n):
    return v.rearrange("p (g o) -> p g o", o=1).to_broadcast([P, n, D])


def over_rows(v, n):
    return v.rearrange("p (o d) -> p o d", o=1).to_broadcast([P, n, D])


def flat(t):
    return t[:].rearrange("p r d -> p (r d)")


def blocks_of(eng, tail):
    return eng.value_load(tail[0:1, 0:1], min_val=1, max_val=TAIL_MAX + 1) + MAIN


ZC = 2048


def clear_table(eng, table, zeros, cleared):
    line = table.rearrange("n d -> (n d)")
    total, at, count = table.shape[0] * table.shape[1], 0, 0
    while at < total:
        n = min(P * ZC, total - at)
        n -= n % P if n > P else 0
        eng.dma_start(line[at:at + n].rearrange("(p c) -> p c", p=P), zeros[:, 0:n // P]).then_inc(cleared, 16)
        at += n
        count += 1
    return count


def gnn_kernel(nc, a, out):
    x = a["x"]
    with ExitStack() as whole:
        def keep(name, shape, dt=F32):
            return whole.enter_context(nc.sbuf_tensor(name, shape, dt))

        meta = [nc.dram_tensor(f"meta{lo}", [S * (MAIN + TAIL_MAX + 1), P, (hi - lo) * G], I32, kind="Internal").ap()
                for lo, hi in PARTS]
        t_mean, t_part, t_z, x1, x2, x3 = (
            nc.dram_tensor(n, [NP, D], F32, kind="Internal").ap() for n in ("t_mean", "t_part", "t_z", "x1", "x2", "x3"))
        t_agg = nc.dram_tensor("t_agg", [AGG_ROWS, D], F32, kind="Internal").ap()

        zeros = keep("zeros", [P, ZC])
        ident = keep("ident", [P, P])
        consts = keep("consts", [P, 4])
        half, one = consts[:, 2:3], consts[:, 1:2]
        tail = keep("tail", [P, 1], I32)
        w = {n: keep("w_" + n, [P, D]) for n in ("g0", "g1", "g2", "c", "g", "in2f", "f2", "o1", "o2", "h3", "c3")}
        w_f1 = keep("w_f1", [RBF, D])
        col = keep("col", [P, 2])
        biases = keep("biases", [P, 4, D])

        prepare(nc, a, meta, zeros, t_mean, ident, consts, tail, w, w_f1, col, biases)
        mean_pass(nc, meta, tail, x, t_mean, zeros, (t_z, t_agg))
        second_mean_pass(nc, meta, tail, x, t_mean, t_part, t_z, ident, w)
        sage_nodes(nc, t_part, t_z, x1, x2)
        mobius_pass(nc, meta, tail, x1, x2, consts)
        schnet_edges(nc, a, x2, t_agg, ident, w, w_f1, col, biases, half, one)
        schnet_nodes(nc, x2, t_agg, x3, out, ident, w, col, biases[:, 2, :], half)
        last_pass(nc, meta, tail, x3, out, ident, w, biases[:, 3, :], consts)


def prepare(nc, a, meta, zeros, t_mean, ident, consts, tail, w, w_f1, col, biases):
    with ExitStack() as ctx:
        sems = []
        ctx.callback(nc.all_engine_barrier)
        ctx.callback(nc.clear_and_free_semaphores, sems)

        def sb(name, shape, dt=F32):
            return ctx.enter_context(nc.sbuf_tensor(name, shape, dt))

        def sem(name):
            sems.append(nc.alloc_semaphore("pre_" + name))
            return sems[-1]

        raw = {n: sb("raw_" + n, [P, D]) for n in ("s0", "n0", "s0t", "n0t", "s1t", "n1t")}
        bcol = sb("bcol", [P, 1])
        brow0 = sb("brow0", [P, D])
        brow1 = sb("brow1", [P, D])
        bwide = sb("bwide", [P, P])
        tmp = sb("tmp", [P, D])
        dwin = sb("dwin", [P, G, C + 2], I32)
        swin = sb("swin", [P, G, C], I32)
        W = sb("W", [P, G, C + 2])
        NS = sb("NS", [P, G, C + 1])
        SM = sb("SM", [P, G, C + 1])
        V, A, T1, RK, T2 = (sb(n, [P, G, C]) for n in ("V", "A", "T1", "RK", "T2"))
        msb = sb("msb", [P, C, FIELDS, G], I32)
        msf = msb[:].bitcast(F32)
        lanes = sb("lanes", [P, 2, G])
        lead = sb("lead", [P, 2])
        allr = sb("allr", [P, 2])
        tl = sb("tl", [P, 1], I32)
        tlf = sb("tlf", [P, 2])
        dwt = sb("dwt", [P, G, S + 2], I32)
        swt = sb("swt", [P, G, S], I32)
        Wt = sb("Wt", [P, G, S + 2])
        NSt = sb("NSt", [P, G, S + 1])
        SMt = sb("SMt", [P, G, S + 1])
        Vt, At, T1t, RKt, T2t = (sb(n, [P, G, S]) for n in ("Vt", "At", "T1t", "RKt", "T2t"))
        mst = sb("mst", [P, S, FIELDS, G], I32)
        mstf = mst[:].bitcast(F32)
        carry = sb("carry", [P, 2, G])
        ps = [ctx.enter_context(nc.psum_tensor(f"pre_ps{k}", [P, 512], F32)) for k in range(4)]

        s_w = sem("weights")
        s_win = sem("window")
        s_zero = sem("zeros")
        s_zeroed = sem("zeroed")
        s_dve = sem("dve")
        s_prod = sem("prod")
        s_wide = sem("wide")
        s_meta = sem("meta")
        s_meta_out = sem("meta_out")
        s_lead = sem("lead")
        s_red = sem("red")
        s_tail = sem("tail")
        s_twin = sem("tail_window")
        s_tmeta = sem("tail_meta")
        s_tout = sem("tail_out")
        s_pool = sem("pool")
        s_hold = sem("hold")

        def window(arr, off, lo, hi):
            return arr[bass.ds(off, LANES * C)].rearrange("(p g c) -> p g c", g=G, c=C)[:, :, lo:hi]

        block = ctx.enter_context(nc.Block())

        @block.sync
        def _(sp):
            sp.dma_start(dwin[:, :, 0:C], window(a["dst_pad"], 0, 0, C)).then_inc(s_win, 16)
            sp.dma_start(dwin[:, :, C:C + 2], window(a["dst_pad"], C, 0, 2)).then_inc(s_win, 16)
            sp.dma_start(swin[:], window(a["src_pad"], 0, 0, C)).then_inc(s_win, 16)
            for n in ("s0", "n0", "s0t", "n0t", "s1t", "n1t"):
                sp.dma_start(raw[n][:], a[n]).then_inc(s_w, 16)
            sp.dma_start(bcol[:], a["b_self0"].rearrange("(p o) -> p o", o=1)).then_inc(s_w, 16)
            sp.dma_start(brow0[:], a["b_self0"].rearrange("(o d) -> o d", o=1).to_broadcast([P, D])).then_inc(s_w, 16)
            sp.dma_start(brow1[:], a["b_self1"].rearrange("(o d) -> o d", o=1).to_broadcast([P, D])).then_inc(s_w, 16)
            for n in ("in2f", "f2", "o1", "o2", "h3", "c3"):
                sp.dma_start(w[n][:], a["w_" + n]).then_inc(s_w, 16)
            sp.dma_start(w_f1[:], a["w_f1"]).then_inc(s_w, 16)
            sp.dma_start(col[:, 0:1], a["b_f1"].rearrange("(p o) -> p o", o=1)).then_inc(s_w, 16)
            sp.dma_start(col[:, 1:2], a["b_o1"].rearrange("(p o) -> p o", o=1)).then_inc(s_w, 16)
            for k, n in enumerate(("b_in2f", "b_f2", "b_o2", "b_3")):
                sp.dma_start(biases[:, k, :], a[n].rearrange("(o d) -> o d", o=1).to_broadcast([P, D])).then_inc(s_w, 16)
            held(sp, s_meta, 1, s_hold)
            for part, (lo, hi) in zip(meta, PARTS):
                sp.dma_start(part[0:C].rearrange("s p f -> p s f"),
                             msb[:, :, lo:hi, :].rearrange("p s f g -> p s (f g)")).then_inc(s_meta_out, 16)
            held(sp, s_tail, 1, s_hold)
            k_tail = sp.value_load(tail[0:1, 0:1], min_val=1, max_val=TAIL_MAX + 1)
            sp.sem_inc(s_tout, CREDIT)
            with sp.Fori(0, k_tail) as k:
                held(sp, s_tmeta, k + CREDIT, s_hold)
                sp.dma_start(dwt[:], window(a["dst_pad"], C + k * S, 0, S + 2)).then_inc(s_twin, 16)
                sp.dma_start(swt[:], window(a["src_pad"], C + k * S, 0, S)).then_inc(s_twin, 16)
                held(sp, s_tmeta, k + 1 + CREDIT, s_hold)
                for part, (lo, hi) in zip(meta, PARTS):
                    sp.dma_start(part[bass.ds(C + S * k, S)].rearrange("s p f -> p s f"),
                                 mst[:, :, lo:hi, :].rearrange("p s f g -> p s (f g)")).then_inc(s_tout, 16)
                held(sp, s_tout, k * 48 + 48 + CREDIT, s_hold)
            held(sp, s_meta_out, 48, s_hold)
            held(sp, s_w, 16 * 22, s_hold)

        @block.scalar
        def _(act):
            act.preload_act_table_set("natural_log_exp_and_others")
            act.wait_ge(s_zero, 1)
            count = clear_table(act, t_mean, zeros, s_zeroed)
            act.wait_ge(s_zeroed, 16 * count)

        @block.gpsimd
        def _(pool):
            pool.memset(ident[:], 0.0).then_inc(s_pool, 1)
            held(pool, s_pool, 1, s_hold)
            pool.affine_select(out=ident[:], in_=ident[:], compare_op=ALU.not_equal, fill=1.0, base=0,
                               pattern=[[-1, P]], channel_multiplier=1).then_inc(s_pool, 1)
            held(pool, s_lead, 1, s_hold)
            pool.partition_all_reduce(allr[:, 0:1], lead[:, 0:1], P, RED.max).then_inc(s_red, 1)
            pool.partition_all_reduce(allr[:, 1:2], lead[:, 1:2], P, RED.add).then_inc(s_red, 1)

        @block.tensor
        def _(pe):
            pe.wait_ge(s_w, 16 * 22)
            pe.matmul(ps[0][:, 0:D], raw["s0"][:], raw["s1t"][:], start=True, stop=True).then_inc(s_prod, 1)
            pe.matmul(ps[1][:, 0:D], raw["n0"][:], raw["s1t"][:], start=True, stop=False)
            pe.matmul(ps[1][:, 0:D], raw["s0"][:], raw["n1t"][:], start=False, stop=True).then_inc(s_prod, 1)
            pe.matmul(ps[2][:, 0:D], raw["n0"][:], raw["n1t"][:], start=True, stop=True).then_inc(s_prod, 1)
            pe.wait_ge(s_wide, 1)
            pe.matmul(ps[3][:, 0:D], bwide[:], raw["s1t"][:], start=True, stop=True).then_inc(s_prod, 1)
            pe.matmul(ps[3][:, D:2 * D], bwide[:], raw["n1t"][:], start=True, stop=True).then_inc(s_prod, 1)

        @block.vector
        def _(dve):
            c = Steps(dve, s_dve)
            dve.memset(zeros[:], 0.0).then_inc(s_zero, 1)
            for k, v in enumerate((EPS_LN, 1.0, 0.5, 0.0)):
                c.do(dve.memset(consts[:, k:k + 1], v))

            def indices(W, NS, SM, V, A, T1, RK, T2, dwin, swin, mi, mf, n, a0, r0, in_tail):
                def m(view, f):
                    return view[:, :, f, :]

                def s3(t, lo, hi):
                    return t[:, :, lo:hi].rearrange("p g c -> p c g")

                c.step(dve.tensor_copy(W[:], dwin[:]))
                c.do(dve.tensor_tensor(NS[:], W[:, :, 0:n + 1], W[:, :, 1:n + 2], ALU.not_equal))
                c.do(dve.tensor_tensor(SM[:], W[:, :, 0:n + 1], W[:, :, 1:n + 2], ALU.is_equal))
                c.step(dve.tensor_scalar(V[:], W[:, :, 1:n + 1], 0.0, None, ALU.is_ge))
                for g in range(G):
                    if in_tail:
                        c.do(dve.tensor_tensor_scan(A[:, g, :], SM[:, g, 0:n], V[:, g, :], a0[:, g:g + 1], ALU.min, ALU.mult))
                    else:
                        c.do(dve.tensor_tensor_scan(A[:, g, :], NS[:, g, 0:n], V[:, g, :], 0.0, ALU.max, ALU.mult))
                c.settle()
                c.step(dve.tensor_tensor(T1[:], SM[:, :, 0:n], A[:], ALU.mult))
                c.do(dve.tensor_copy(m(mf, CONT), s3(T1, 0, n)))
                for g in range(G):
                    c.do(dve.tensor_tensor_scan(RK[:, g, :], T1[:, g, :], T1[:, g, :], r0[:, g:g + 1] if in_tail else 0.0,
                                                ALU.mult, ALU.add))
                c.settle()
                c.step(dve.tensor_scalar(T2[:], RK[:], 1.0, None, ALU.add))
                c.step(dve.reciprocal(m(mf, RDEG), s3(T2, 0, n)))
                c.do(dve.tensor_tensor(m(mi, DST), s3(W, 1, n + 1), s3(A, 0, n), ALU.mult))
                c.step(dve.tensor_copy(T2[:], swin[:]))
                c.do(dve.tensor_tensor(m(mi, SRC), s3(T2, 0, n), s3(A, 0, n), ALU.mult))
                c.step(dve.tensor_tensor(T1[:], A[:], NS[:, :, 1:n + 1], ALU.mult))
                c.step(dve.scalar_tensor_tensor(T2[:], W[:, :, 1:n + 1], -float(NP), T1[:], ALU.add, ALU.mult))
                c.do(dve.tensor_scalar(m(mi, OUT), s3(T2, 0, n), float(NP), None, ALU.add))

            dve.wait_ge(s_win, 48)
            indices(W, NS, SM, V, A, T1, RK, T2, dwin, swin, msb, msf, C, 0.0, 0.0, False)
            c.settle()
            c.step(dve.tensor_copy(carry[:, 0, :], A[:, :, C - 1]))
            dve.tensor_copy(carry[:, 1, :], RK[:, :, C - 1]).then_inc(s_meta, 1)
            c.step(dve.tensor_tensor(T1[:], V[:], A[:], ALU.subtract))
            c.step(dve.tensor_reduce(lanes[:, 0, :], T1[:], AX, ALU.add))
            c.do(dve.tensor_reduce(lead[:, 0:1], lanes[:, 0, :], AX, ALU.max))
            c.step(dve.tensor_scalar(lanes[:, 1, :], lanes[:, 0, :], float(C), float(C), ALU.is_ge, ALU.mult))
            dve.tensor_reduce(lead[:, 1:2], lanes[:, 1, :], AX, ALU.add).then_inc(s_lead, 1)
            dve.wait_ge(s_red, 2)
            c.step(dve.tensor_tensor(lead[:, 0:1], allr[:, 0:1], allr[:, 1:2], ALU.add))
            c.step(dve.tensor_scalar(tl[:], lead[:, 0:1], 1.0 / S, None, ALU.mult))
            c.step(dve.tensor_copy(tlf[:, 0:1], tl[:]))
            c.step(dve.tensor_scalar(tlf[:, 1:2], tlf[:, 0:1], float(S), None, ALU.mult))
            c.step(dve.tensor_tensor(tlf[:, 1:2], tlf[:, 1:2], lead[:, 0:1], ALU.is_lt))
            c.step(dve.tensor_tensor(tlf[:, 0:1], tlf[:, 0:1], tlf[:, 1:2], ALU.add))
            dve.tensor_scalar(tail[:], tlf[:, 0:1], 1.0, float(TAIL_MAX), ALU.max, ALU.min).then_inc(s_tail, 1)
            dve.wait_ge(s_tail, 1)
            k_tail = dve.value_load(tail[0:1, 0:1], min_val=1, max_val=TAIL_MAX + 1)
            c.restart()
            dve.sem_inc(s_tmeta, CREDIT)
            with dve.Fori(0, k_tail) as k:
                dve.wait_ge(s_twin, k * 32 + 32)
                dve.wait_ge(s_tout, k * 48 + CREDIT)
                indices(Wt, NSt, SMt, Vt, At, T1t, RKt, T2t, dwt, swt, mst, mstf, S, carry[:, 0, :], carry[:, 1, :], True)
                c.settle()
                c.step(dve.tensor_copy(carry[:, 0, :], At[:, :, S - 1]))
                c.step(dve.tensor_copy(carry[:, 1, :], RKt[:, :, S - 1]))
                c.restart()
                dve.sem_inc(s_tmeta, 1)
            dve.wait_ge(s_w, 16 * 22)
            c.step(dve.tensor_copy(bwide[:], bcol[:, 0:1].to_broadcast([P, P])))
            dve.sem_inc(s_wide, 1)
            dve.wait_ge(s_prod, 5)
            dve.wait_ge(s_pool, 2)
            c.step(dve.scalar_tensor_tensor(tmp[:], ps[0][:, 0:D], 0.5, raw["s0t"][:], ALU.mult, ALU.add))
            c.do(dve.scalar_tensor_tensor(w["g0"][:], ident[:], 2.0, tmp[:], ALU.mult, ALU.add))
            c.do(dve.scalar_tensor_tensor(w["g1"][:], ps[1][:, 0:D], 0.5, raw["n0t"][:], ALU.mult, ALU.add))
            c.do(dve.tensor_scalar(w["g2"][:], ps[2][:, 0:D], 0.5, None, ALU.mult))
            c.do(dve.tensor_scalar(w["g"][:], ps[3][:, D:2 * D], 0.5, None, ALU.mult))
            c.step(dve.tensor_tensor(brow1[:], brow1[:], ps[3][:, 0:D], ALU.add))
            c.step(dve.scalar_tensor_tensor(w["c"][:], brow1[:], 0.5, brow0[:], ALU.mult, ALU.add))


def load_meta(sp, mt, meta, b, u, scattered, meta_in, s_hold):
    if not (isinstance(b, int) and b == 0):
        held(sp, scattered[u], b * (16 * G), s_hold)
    for part, (lo, hi) in zip(meta, PARTS):
        sp.dma_start(mt[u][:, lo:hi, :].rearrange("p f g -> p (f g)"),
                     part[bass.ds(b * S + u, 1)].rearrange("a p f -> p (a f)")).then_inc(meta_in[u], 16)


def gather_rows(pool, table, mt, field, to, gathered):
    for g in range(G):
        pool.indirect_dma_start(out=to[:, g, :], out_offset=None, in_=table,
                                in_offset=bass.IndirectOffsetOnAxis(ap=mt[:, field, g:g + 1], axis=0),
                                bounds_check=N - 1, oob_is_err=False).then_inc(gathered, 16)


def scatter_rows(pool, table, mt, rows, scattered):
    for g in range(G):
        pool.indirect_dma_start(out=table, out_offset=bass.IndirectOffsetOnAxis(ap=mt[:, OUT, g:g + 1], axis=0),
                                in_=rows[:, g, :], in_offset=None,
                                bounds_check=N - 1, oob_is_err=False).then_inc(scattered, 16)


def mean_pass(nc, meta, tail, source, table, zeros, tables):
    with ExitStack() as ctx:
        sems = []
        ctx.callback(nc.all_engine_barrier)
        ctx.callback(nc.clear_and_free_semaphores, sems)

        def sb(n, shape, dt=F32):
            return ctx.enter_context(nc.sbuf_tensor("mean_" + n, shape, dt))

        def sem(n):
            sems.append(nc.alloc_semaphore("mean_" + n))
            return sems[-1]

        mt = [sb(f"mt{u}", [P, FIELDS, G], I32) for u in range(S)]
        mf = [t[:].bitcast(F32) for t in mt]
        msg, run, row = ([sb(f"{n}{u}", [P, G, D]) for u in range(S)] for n in ("msg", "run", "row"))
        meta_in, gathered, scattered = ([sem(f"{n}{u}") for u in range(S)] for n in ("meta_in", "gathered", "scattered"))
        s_sum, s_row, s_hold, s_zeroed = sem("sum"), sem("row"), sem("hold"), sem("zeroed")
        block = ctx.enter_context(nc.Block())

        @block.sync
        def _(sp):
            n = blocks_of(sp, tail)
            pipeline(n, S, sp, [(0, lambda b, u: load_meta(sp, mt, meta, b, u, scattered, meta_in, s_hold))])
            for u in range(S):
                held(sp, scattered[u], n * (16 * G), s_hold)

        @block.gpsimd
        def _(pool):
            def gather(b, u):
                held(pool, meta_in[u], b * 48 + 48, s_hold)
                gather_rows(pool, source, mt[u], SRC, msg[u], gathered[u])

            def scatter(b, u):
                held(pool, s_row, done(b * S + u), s_hold)
                scatter_rows(pool, table, mt[u], row[u], scattered[u])

            pipeline(blocks_of(pool, tail), S, pool, [(0, gather), (3, scatter)])

        @block.vector
        def _(dve):
            n = blocks_of(dve, tail)
            dve.memset(run[S - 1][:], 0.0).then_inc(s_sum, CREDIT)
            with dve.Fori(0, n) as b:
                for u in range(S):
                    dve.wait_ge(gathered[u], b * (16 * G) + 16 * G)
                    dve.wait_ge(s_row, freed(b * S + u, S))
                    dve.wait_ge(s_sum, done(b * S + u - 1))
                    for g in range(G):
                        ins = dve.scalar_tensor_tensor(run[u][:, g, :], run[u - 1][:, g, :], mf[u][:, CONT, g:g + 1],
                                                       msg[u][:, g, :], ALU.mult, ALU.add)
                    ins.then_inc(s_sum, 1)

        @block.scalar
        def _(act):
            n = blocks_of(act, tail)
            act.sem_inc(s_row, CREDIT)
            count = sum(clear_table(act, t[NP:], zeros, s_zeroed) for t in tables if t.shape[0] > NP)

            def clear(b, u):
                rows = NP // C
                for t in tables:
                    act.dma_start(t[bass.ds((b * S + u) * rows, rows)].rearrange("(p r) d -> p (r d)", p=P),
                                  zeros[:, 0:rows * D // P]).then_inc(s_zeroed, 16)

            def scale(b, u):
                act.wait_ge(s_sum, done(b * S + u))
                act.wait_ge(meta_in[u], b * 48 + 48)
                for g in range(G):
                    ins = act.activation(row[u][:, g, :], run[u][:, g, :], ACT.Copy, scale=mf[u][:, RDEG, g:g + 1])
                ins.then_inc(s_row, 1)

            pipeline(n, S, act, [(0, clear, True), (0, scale)], MAIN)
            act.wait_ge(s_zeroed, 16 * (count + len(tables) * C))


def second_mean_pass(nc, meta, tail, x, t_mean, t_part, t_z, ident, w):
    with ExitStack() as ctx:
        sems = []
        ctx.callback(nc.all_engine_barrier)
        ctx.callback(nc.clear_and_free_semaphores, sems)

        def sb(n, shape, dt=F32):
            return ctx.enter_context(nc.sbuf_tensor("two_" + n, shape, dt))

        def sem(n):
            sems.append(nc.alloc_semaphore("two_" + n))
            return sems[-1]

        H = range(WITH)
        mt = [sb(f"mt{u}", [P, FIELDS, G], I32) for u in range(S)]
        mf = [t[:].bitcast(F32) for t in mt]
        msg, run, row, zr = ([sb(f"{n}{u}", [P, G, D]) for u in range(S)] for n in ("msg", "run", "row", "zr"))
        rt = sb("rt", [P, G * P])
        xi, mi, vo = ([[sb(f"{n}{u}{h}", [P, NB, D]) for h in H] for u in range(S)] for n in ("xi", "mi", "vo"))
        xt, mtr = ([sb(f"{n}{h}", [P, BN]) for h in H] for n in ("xt", "mtr"))
        p_x, p_m, p_v = ([ctx.enter_context(nc.psum_tensor(f"two_{n}{h}", [P, BN], F32)) for h in H] for n in "xmv")
        p_r, p_z = (ctx.enter_context(nc.psum_tensor(f"two_{n}", [P, BN], F32)) for n in ("pr", "pz"))
        meta_in, gathered, scattered, loaded, stored = (
            [sem(f"{n}{u}") for u in range(S)] for n in ("meta_in", "gathered", "scattered", "loaded", "stored"))
        s_trx, s_xt, s_mt, s_vm, s_v = ([sem(f"{n}{h}") for h in H] for n in ("trx", "xt", "mt", "vm", "v"))
        s_sum, s_row, s_hold, s_trr, s_rt, s_zm, s_z = (sem(n) for n in ("sum", "row", "hold", "trr", "rt", "zm", "z"))
        block = ctx.enter_context(nc.Block())

        def step(b, u):
            return b * S + u

        def batch(b, u, h):
            return (b * S + u) * WITH + h

        @block.sync
        def _(sp):
            n = blocks_of(sp, tail)
            for s in stored:
                sp.sem_inc(s, CREDIT)

            def load_column(b, u):
                load_meta(sp, mt, meta, b, u, scattered, meta_in, s_hold)

            def load_nodes(b, u):
                for h in H:
                    held(sp, s_trx[h], freed(step(b, u), S), s_hold)
                for h in H:
                    sp.dma_start(flat(xi[u][h]), node_view(x, batch(b, u, h))).then_inc(loaded[u], 16)
                    sp.dma_start(flat(mi[u][h]), node_view(t_mean, batch(b, u, h))).then_inc(loaded[u], 16)

            def store_nodes(b, u):
                for h in H:
                    held(sp, s_v[h], done(step(b, u)), s_hold)
                    sp.dma_start(node_view(t_part, batch(b, u, h)), flat(vo[u][h])).then_inc(stored[u], 16)

            pipeline(MAIN, S, sp, [(0, load_column), (0, load_nodes), (4, store_nodes)])
            with sp.Fori(MAIN, n) as b:
                for u in range(S):
                    load_column(b, u)
            for u in range(S):
                held(sp, scattered[u], n * (16 * G), s_hold)
                held(sp, stored[u], MAIN * (16 * WITH) + CREDIT, s_hold)

        @block.gpsimd
        def _(pool):
            def gather(b, u):
                held(pool, meta_in[u], b * 48 + 48, s_hold)
                gather_rows(pool, t_mean, mt[u], SRC, msg[u], gathered[u])

            def scatter(b, u):
                held(pool, s_z, done(step(b, u)), s_hold)
                scatter_rows(pool, t_z, mt[u], zr[u], scattered[u])

            pipeline(blocks_of(pool, tail), S, pool, [(0, gather), (3, scatter)])

        @block.tensor
        def _(pe):
            for s in (*s_trx, *s_vm, s_trr, s_zm):
                pe.sem_inc(s, CREDIT)

            def transpose_nodes(b, u):
                pe.wait_ge(loaded[u], b * (32 * WITH) + 32 * WITH)
                for h in H:
                    pe.wait_ge(s_xt[h], freed(step(b, u), 1))
                    pe.wait_ge(s_mt[h], freed(step(b, u), 1))
                    for src, bank in ((xi, p_x), (mi, p_m)):
                        for j in range(NB):
                            ins = pe.transpose(bank[h][:, j * P:(j + 1) * P], src[u][h][:, j, :], ident[:])
                    ins.then_inc(s_trx[h], 1)

            def node_products(b, u):
                for h in H:
                    pe.wait_ge(s_xt[h], done(step(b, u)))
                    pe.wait_ge(s_mt[h], done(step(b, u)))
                    pe.wait_ge(s_v[h], freed(step(b, u), 1))
                    for j in range(NB):
                        pe.matmul(p_v[h][:, j * D:(j + 1) * D], xt[h][:, j * P:(j + 1) * P], w["g0"][:], start=True, stop=False)
                        ins = pe.matmul(p_v[h][:, j * D:(j + 1) * D], mtr[h][:, j * P:(j + 1) * P], w["g1"][:],
                                        start=False, stop=True)
                    ins.then_inc(s_vm[h], 1)

            def transpose_rows(b, u):
                pe.wait_ge(s_row, done(step(b, u)))
                pe.wait_ge(s_rt, freed(step(b, u), 1))
                for g in range(G):
                    ins = pe.transpose(p_r[:, g * P:(g + 1) * P], row[u][:, g, :], ident[:])
                ins.then_inc(s_trr, 1)

            def row_products(b, u):
                pe.wait_ge(s_rt, done(step(b, u)))
                pe.wait_ge(s_z, freed(step(b, u), 1))
                for g in range(G):
                    ins = pe.matmul(p_z[:, g * D:(g + 1) * D], rt[:, g * P:(g + 1) * P], w["g2"][:], start=True, stop=True)
                ins.then_inc(s_zm, 1)

            pipeline(blocks_of(pe, tail), S, pe,
                     [(0, transpose_nodes, True), (1, transpose_rows), (0, node_products, True), (1, row_products)], MAIN)

        @block.scalar
        def _(act):
            for s in (*s_xt, s_row, s_rt):
                act.sem_inc(s, CREDIT)

            def copy_nodes(b, u):
                for h in H:
                    act.wait_ge(s_trx[h], done(step(b, u)))
                    act.wait_ge(s_vm[h], freed(step(b, u), 1))
                    act.activation(xt[h][:], p_x[h][:], ACT.Copy).then_inc(s_xt[h], 1)

            def copy_rows(b, u):
                act.wait_ge(s_trr, done(step(b, u)))
                act.wait_ge(s_zm, freed(step(b, u), 1))
                act.activation(rt[:], p_r[:], ACT.Copy).then_inc(s_rt, 1)

            def scale(b, u):
                act.wait_ge(s_sum, done(step(b, u)))
                act.wait_ge(s_trr, freed(step(b, u), S))
                act.wait_ge(meta_in[u], b * 48 + 48)
                for g in range(G):
                    ins = act.activation(row[u][:, g, :], run[u][:, g, :], ACT.Copy, scale=mf[u][:, RDEG, g:g + 1])
                ins.then_inc(s_row, 1)

            pipeline(blocks_of(act, tail), S, act, [(0, copy_nodes, True), (1, copy_rows), (0, scale)], MAIN)

        @block.vector
        def _(dve):
            dve.memset(run[S - 1][:], 0.0).then_inc(s_sum, CREDIT)
            for s in (*s_mt, *s_v, s_z):
                dve.sem_inc(s, CREDIT)

            def copy_nodes(b, u):
                for h in H:
                    dve.wait_ge(s_trx[h], done(step(b, u)))
                    dve.wait_ge(s_vm[h], freed(step(b, u), 1))
                    dve.tensor_copy(mtr[h][:], p_m[h][:]).then_inc(s_mt[h], 1)

            def sums(b, u):
                dve.wait_ge(gathered[u], b * (16 * G) + 16 * G)
                dve.wait_ge(s_row, freed(step(b, u), S))
                dve.wait_ge(s_sum, done(step(b, u) - 1))
                for g in range(G):
                    ins = dve.scalar_tensor_tensor(run[u][:, g, :], run[u - 1][:, g, :], mf[u][:, CONT, g:g + 1],
                                                   msg[u][:, g, :], ALU.mult, ALU.add)
                ins.then_inc(s_sum, 1)

            def node_values(b, u):
                dve.wait_ge(stored[u], b * (16 * WITH) + CREDIT)
                for h in H:
                    dve.wait_ge(s_vm[h], done(step(b, u)))
                    dve.tensor_tensor(vo[u][h][:], p_v[h][:].rearrange("p (r d) -> p r d", r=NB), over_rows(w["c"][:], NB),
                                      ALU.add).then_inc(s_v[h], 1)

            def row_values(b, u):
                dve.wait_ge(s_zm, done(step(b, u)))
                dve.wait_ge(meta_in[u], b * 48 + 48)
                dve.tensor_tensor(zr[u][:], p_z[:].rearrange("p (g d) -> p g d", g=G), over_rows(w["g"][:], G),
                                  ALU.add).then_inc(s_z, 1)

            pipeline(blocks_of(dve, tail), S, dve,
                     [(0, copy_nodes, True), (0, sums), (0, node_values, True), (1, row_values)], MAIN)


def node_view(table, t, width=D):
    return table[bass.ds(t * BN, BN)].rearrange("(p r) d -> p (r d)", p=P)


def norm_factors_begin(dve, c, v, st, mv, arg):
    for j in range(NB):
        c.do(dve.bn_stats(out=st[:, j, :], in_=v[:, j, :]))
    c.settle()
    for j in range(NB):
        c.do(dve.bn_aggr(out=mv[:, j, :], in_=st[:, j, :]))
    c.settle()
    c.do(dve.tensor_scalar(arg[:, 0, :], mv[:, :, 1], EPS_LN, None, ALU.add))
    c.do(dve.tensor_scalar(arg[:, 1, :], mv[:, :, 1], 1.0 + EPS_LN / 4, EPS_LN * EPS_LN / 4, ALU.mult, ALU.add))
    c.settle()
    c.step(dve.reciprocal(arg[:, 2, :], arg[:, 0, :]))
    return dve.tensor_tensor(arg[:, 1, :], arg[:, 1, :], arg[:, 2, :], ALU.mult)


def norm_factors_root(act, c, arg, rs):
    c.step(act.activation(rs[:, 0:2, :], arg[:, 0:2, :], ACT.Ln))
    return act.activation(rs[:, 0:2, :], rs[:, 0:2, :], ACT.Exp, scale=-0.5)


def sage_nodes(nc, t_part, t_z, x1, x2):
    with ExitStack() as ctx:
        sems = []
        ctx.callback(nc.all_engine_barrier)
        ctx.callback(nc.clear_and_free_semaphores, sems)

        def sb(n, shape, dt=F32):
            return ctx.enter_context(nc.sbuf_tensor("sage_" + n, shape, dt))

        def sem(n):
            sems.append(nc.alloc_semaphore("sage_" + n))
            return sems[-1]

        part, z, v, o1, o2 = ([sb(f"{n}{u}", [P, NB, D]) for u in range(SN)] for n in ("part", "z", "v", "o1", "o2"))
        st = [sb(f"st{u}", [P, NB, 6]) for u in range(SN)]
        mv = [sb(f"mv{u}", [P, NB, 2]) for u in range(SN)]
        rs, arg = ([sb(f"{n}{u}", [P, 3, NB]) for u in range(SN)] for n in ("rs", "arg"))
        loaded, stored = ([sem(f"{n}{u}") for u in range(SN)] for n in ("loaded", "stored"))
        s_v, s_st, s_rs, s_nb, s_o1, s_o2 = (sem(k) for k in ("v", "st", "rs", "nb", "o1", "o2"))
        s_dve, s_act, s_hold = sem("dve"), sem("act"), sem("hold")
        IT = BATCHES // SN
        block = ctx.enter_context(nc.Block())

        @block.sync
        def _(sp):
            def load(i, u):
                held(sp, s_v, freed(i * SN + u, SN), s_hold)
                sp.dma_start(flat(part[u]), node_view(t_part, i * SN + u)).then_inc(loaded[u], 16)
                sp.dma_start(flat(z[u]), node_view(t_z, i * SN + u)).then_inc(loaded[u], 16)

            pipeline(IT, SN, sp, [(0, load)])

        @block.scalar
        def _(act):
            act.preload_act_table_set("natural_log_exp_and_others")
            c = Steps(act, s_act)
            act.sem_inc(s_rs, CREDIT)
            act.sem_inc(s_o1, CREDIT)
            for u in range(SN):
                act.sem_inc(stored[u], CREDIT)

            def roots(i, u):
                t = i * SN + u
                act.wait_ge(s_st, done(t))
                act.wait_ge(s_o2, freed(t, SN))
                norm_factors_root(act, c, arg[u], rs[u]).then_inc(s_rs, 1)
                c.restart()

            def norm(i, u):
                t = i * SN + u
                act.wait_ge(s_nb, done(t))
                act.wait_ge(stored[u], i * 32 + CREDIT)
                for j in range(NB):
                    ins = act.activation(o1[u][:, j, :], v[u][:, j, :], ACT.Identity, bias=rs[u][:, 2, j:j + 1], scale=rs[u][:, 0, j:j + 1])
                ins.then_inc(s_o1, 1)

            def store(i, u):
                t = i * SN + u
                act.wait_ge(s_o1, done(t))
                act.dma_start(node_view(x1, t), flat(o1[u])).then_inc(stored[u], 16)
                act.wait_ge(s_o2, done(t))
                act.dma_start(node_view(x2, t), flat(o2[u])).then_inc(stored[u], 16)

            pipeline(IT, SN, act, [(0, roots), (3, store), (1, norm)])
            for u in range(SN):
                act.wait_ge(stored[u], 32 * IT + CREDIT)

        @block.vector
        def _(dve):
            c = Steps(dve, s_dve)
            for s in (s_v, s_st, s_nb):
                dve.sem_inc(s, CREDIT)

            def values(i, u):
                t = i * SN + u
                dve.wait_ge(loaded[u], i * 32 + 32)
                dve.wait_ge(s_o1, freed(t, SN))
                dve.tensor_tensor(v[u][:], part[u][:], z[u][:], ALU.add).then_inc(s_v, 1)
                dve.wait_ge(s_v, done(t))
                norm_factors_begin(dve, c, v[u], st[u], mv[u], arg[u]).then_inc(s_st, 1)
                c.restart()

            def bias(i, u):
                dve.wait_ge(s_rs, done(i * SN + u))
                dve.scalar_tensor_tensor(rs[u][:, 2, :], mv[u][:, :, 0], -1.0, rs[u][:, 0, :], ALU.mult, ALU.mult).then_inc(s_nb, 1)

            pipeline(IT, SN, dve, [(0, values), (1, bias)])

        @block.gpsimd
        def _(pool):
            pool.sem_inc(s_o2, CREDIT)

            def double(i, u):
                held(pool, s_o1, done(i * SN + u), s_hold)
                held(pool, stored[u], i * 32 + CREDIT, s_hold)
                pool.tensor_tensor(o2[u][:], o1[u][:], lanes_of(rs[u][:, 1, :], NB), ALU.mult).then_inc(s_o2, 1)

            pipeline(IT, SN, pool, [(0, double)])


def mobius_pass(nc, meta, tail, x1, x2, consts):
    with ExitStack() as ctx:
        sems = []
        ctx.callback(nc.all_engine_barrier)
        ctx.callback(nc.clear_and_free_semaphores, sems)

        def sb(n, shape, dt=F32):
            return ctx.enter_context(nc.sbuf_tensor("mob_" + n, shape, dt))

        def sem(n):
            sems.append(nc.alloc_semaphore("mob_" + n))
            return sems[-1]

        mt = [sb(f"mt{u}", [P, FIELDS, G], I32) for u in range(S)]
        mf = [t[:].bitcast(F32) for t in mt]
        xs, xd, msg, run, v, row = ([sb(f"{n}{u}", [P, G, D]) for u in range(S)] for n in ("xs", "xd", "msg", "run", "v", "row"))
        prod_m, prod_s, prod_v = (sb(f"prod_{k}", [P, G, D]) for k in "msv")
        junk = sb("junk", [P, 4, G, D])
        nrm = [sb(f"nrm{u}", [P, 4, G]) for u in range(S)]
        q = [sb(f"q{u}", [P, 22, G]) for u in range(S)]
        sc = sb("sc", [P, 10, G])
        lg = [sb(f"lg{u}", [P, 5, G]) for u in range(S)]
        st = [sb(f"st{u}", [P, G, 6]) for u in range(S)]
        mv = [sb(f"mv{u}", [P, G, 2]) for u in range(S)]
        rs = [sb(f"rs{u}", [P, 3, G]) for u in range(S)]
        eps_ln, one = consts[:, 0:1], consts[:, 1:2]

        meta_in, gathered, scattered = ([sem(f"{n}{u}") for u in range(S)] for n in ("meta_in", "gathered", "scattered"))
        s_sq, s_ab, s_part, s_msg, s_msq, s_run, s_rsq, s_log, s_arg, s_exp, s_cd, s_vc, s_vpart, s_st, s_rs, s_nb, s_row = (
            sem(k) for k in ("sq", "ab", "part", "msg", "msq", "run", "rsq", "log", "arg", "exp", "cd", "vc", "vpart", "st", "rs",
                             "nb", "row"))
        s_dve, s_act, s_hold = sem("dve"), sem("act"), sem("hold")
        block = ctx.enter_context(nc.Block())

        @block.sync
        def _(sp):
            n = blocks_of(sp, tail)
            pipeline(n, S, sp, [(0, lambda b, u: load_meta(sp, mt, meta, b, u, scattered, meta_in, s_hold))])
            for u in range(S):
                held(sp, scattered[u], n * (16 * G), s_hold)

        @block.gpsimd
        def _(pool):
            def gather(b, u):
                held(pool, meta_in[u], b * 48 + 48, s_hold)
                gather_rows(pool, x1, mt[u], SRC, xs[u], gathered[u])
                gather_rows(pool, x1, mt[u], DST, xd[u], gathered[u])

            def scatter(b, u):
                held(pool, s_row, done(b * S + u), s_hold)
                scatter_rows(pool, x2, mt[u], row[u], scattered[u])

            pipeline(blocks_of(pool, tail), S, pool, [(0, gather), (5, scatter)])

        @block.scalar
        def _(act):
            act.preload_act_table_set("natural_log_exp_and_others")
            c = Steps(act, s_act)
            for s in (s_sq, s_part, s_msq, s_rsq, s_log, s_exp, s_vpart, s_rs, s_row):
                act.sem_inc(s, CREDIT)

            def square(k, src, u):
                for g in range(G):
                    ins = act.activation(junk[:, k, g, :], src[u][:, g, :], ACT.Square, accum_out=nrm[u][:, k, g:g + 1])
                return ins

            def squares(b, u):
                t = b * S + u
                act.wait_ge(gathered[u], b * (32 * G) + 32 * G)
                act.wait_ge(s_nb, freed(t, S))
                act.wait_ge(s_sq, done(t - 1))
                square(0, xs, u)
                square(1, xd, u).then_inc(s_sq, 1)

            def message_part(b, u):
                act.wait_ge(s_ab, done(b * S + u))
                for g in range(G):
                    ins = act.activation(msg[u][:, g, :], xd[u][:, g, :], ACT.Copy, scale=q[u][:, 7, g:g + 1])
                ins.then_inc(s_part, 1)

            def message_square(b, u):
                act.wait_ge(s_msg, done(b * S + u))
                act.wait_ge(s_msq, done(b * S + u - 1))
                square(2, msg, u).then_inc(s_msq, 1)

            def run_square(b, u):
                act.wait_ge(s_run, done(b * S + u))
                act.wait_ge(s_rsq, done(b * S + u - 1))
                square(3, run, u).then_inc(s_rsq, 1)

            def logs(b, u):
                act.wait_ge(s_cd, done(b * S + u))
                c.step(act.activation(lg[u][:, 1, :], lg[u][:, 0, :], ACT.Ln))
                c.step(act.activation(lg[u][:, 2, :], lg[u][:, 1, :], ACT.Exp, scale=0.5))
                c.do(act.activation(lg[u][:, 4, :], lg[u][:, 0, :], ACT.Ln, bias=one, scale=-1.0))
                act.activation(lg[u][:, 3, :], lg[u][:, 2, :], ACT.Ln, bias=one).then_inc(s_log, 1)
                c.restart()

            def exps(b, u):
                act.wait_ge(s_arg, done(b * S + u))
                act.activation(q[u][:, 10, :], q[u][:, 9, :], ACT.Exp).then_inc(s_exp, 1)

            def value_part(b, u):
                act.wait_ge(s_vc, done(b * S + u))
                for g in range(G):
                    ins = act.activation(v[u][:, g, :], run[u][:, g, :], ACT.Copy, scale=q[u][:, 21, g:g + 1])
                ins.then_inc(s_vpart, 1)

            def rstd(b, u):
                act.wait_ge(s_st, done(b * S + u))
                c.step(act.activation(rs[u][:, 0, :], mv[u][:, :, 1], ACT.Ln, bias=eps_ln))
                act.activation(rs[u][:, 1, :], rs[u][:, 0, :], ACT.Exp, scale=-0.5).then_inc(s_rs, 1)
                c.restart()

            def norm(b, u):
                act.wait_ge(s_nb, done(b * S + u))
                act.wait_ge(meta_in[u], b * 48 + 48)
                for g in range(G):
                    ins = act.activation(row[u][:, g, :], v[u][:, g, :], ACT.Identity, bias=rs[u][:, 2, g:g + 1], scale=rs[u][:, 1, g:g + 1])
                ins.then_inc(s_row, 1)

            pipeline(blocks_of(act, tail), S, act,
                     [(4, exps), (1, message_part), (4, value_part), (1, message_square), (4, rstd), (3, logs),
                      (0, squares), (2, run_square), (4, norm)])

        @block.vector
        def _(dve):
            c = Steps(dve, s_dve)
            c.do(dve.memset(run[S - 1][:], 0.0))
            c.step(dve.memset(nrm[S - 1][:, 3, :], 0.0))
            c.restart()
            for s in (s_ab, s_msg, s_run, s_cd, s_arg, s_st, s_vc, s_nb):
                dve.sem_inc(s, CREDIT)
            ts, tt, stt = dve.tensor_scalar, dve.tensor_tensor, dve.scalar_tensor_tensor

            def message_factors(b, u):
                dve.wait_ge(gathered[u], b * (32 * G) + 32 * G)
                dve.wait_ge(s_row, freed(b * S + u, S))
                k = q[u]
                dve.wait_ge(s_sq, done(b * S + u))
                c.do(tt(k[:, 2, :], nrm[u][:, 0, :], nrm[u][:, 1, :], ALU.mult))
                for g in range(G):
                    c.do(dve.tensor_tensor_reduce(out=prod_m[:, g, :], in0=xs[u][:, g, :], in1=xd[u][:, g, :], scale=1.0,
                                                  scalar=0.0, op0=ALU.mult, op1=ALU.add, accum_out=k[:, 0, g:g + 1]))
                c.settle()
                c.do(ts(k[:, 1, :], k[:, 0, :], -2.0, 1.0, ALU.mult, ALU.add))
                c.settle()
                c.step(tt(k[:, 2, :], k[:, 2, :], k[:, 1, :], ALU.add))
                c.do(tt(k[:, 3, :], k[:, 1, :], nrm[u][:, 1, :], ALU.add))
                c.step(ts(k[:, 2, :], k[:, 2, :], EPS, None, ALU.max))
                c.step(dve.reciprocal(k[:, 5, :], k[:, 2, :]))
                c.do(tt(k[:, 6, :], k[:, 3, :], k[:, 5, :], ALU.mult))
                stt(k[:, 7, :], nrm[u][:, 0, :], -1.0, k[:, 5, :], ALU.add, ALU.mult).then_inc(s_ab, 1)

            def messages(b, u):
                c.settle()
                dve.wait_ge(s_part, done(b * S + u))
                for g in range(G):
                    ins = stt(msg[u][:, g, :], xs[u][:, g, :], q[u][:, 6, g:g + 1], msg[u][:, g, :], ALU.mult, ALU.add)
                ins.then_inc(s_msg, 1)

            def scan(b, u):
                t = b * S + u
                dve.wait_ge(s_msq, done(t))
                dve.wait_ge(s_run, done(t - 1))
                prev, cont, m2 = run[u - 1], mf[u][:, CONT, :], nrm[u][:, 2, :]
                if not (isinstance(b, int) and b == 0 and u == 0):
                    dve.wait_ge(s_rsq, done(t - 1))
                c.do(tt(sc[:, 1, :], nrm[u - 1][:, 3, :], cont, ALU.mult))
                for g in range(G):
                    c.do(dve.tensor_tensor_reduce(out=prod_s[:, g, :], in0=prev[:, g, :], in1=msg[u][:, g, :], scale=1.0,
                                                  scalar=0.0, op0=ALU.mult, op1=ALU.add, accum_out=sc[:, 0, g:g + 1]))
                c.settle(but=G)
                c.do(ts(sc[:, 6, :], sc[:, 1, :], -1.0, 1.0, ALU.mult, ALU.add))
                c.do(tt(sc[:, 4, :], sc[:, 1, :], m2, ALU.mult))
                c.settle(but=2)
                c.step(stt(sc[:, 2, :], sc[:, 0, :], 2.0, cont, ALU.mult, ALU.mult))
                c.do(stt(sc[:, 3, :], sc[:, 2, :], 1.0, m2, ALU.add, ALU.add))
                c.step(stt(sc[:, 5, :], sc[:, 2, :], 1.0, sc[:, 4, :], ALU.add, ALU.add))
                c.step(ts(sc[:, 5, :], sc[:, 5, :], EPS, None, ALU.max))
                c.do(tt(sc[:, 3, :], sc[:, 3, :], cont, ALU.mult))
                c.step(dve.reciprocal(sc[:, 7, :], sc[:, 5, :]))
                c.do(tt(sc[:, 9, :], sc[:, 6, :], sc[:, 7, :], ALU.mult))
                c.step(tt(sc[:, 8, :], sc[:, 3, :], sc[:, 7, :], ALU.mult))
                c.step(tt(prod_s[:], prev[:], lanes_of(sc[:, 8, :], G), ALU.mult))
                for g in range(G):
                    ins = stt(run[u][:, g, :], msg[u][:, g, :], sc[:, 9, g:g + 1], prod_s[:, g, :], ALU.mult, ALU.add)
                ins.then_inc(s_run, 1)

            def clip(b, u):
                dve.wait_ge(s_rsq, done(b * S + u))
                ts(lg[u][:, 0, :], nrm[u][:, 3, :], EPS * EPS, ONE_MINUS_SQ, ALU.max, ALU.min).then_inc(s_cd, 1)

            def arguments(b, u):
                dve.wait_ge(s_log, done(b * S + u))
                k = q[u]
                c.step(stt(k[:, 8, :], lg[u][:, 3, :], 2.0, lg[u][:, 4, :], ALU.mult, ALU.subtract))
                tt(k[:, 9, :], k[:, 8, :], mf[u][:, RDEG, :], ALU.mult).then_inc(s_arg, 1)

            def value_factors(b, u):
                k = q[u]
                r2, x2n = nrm[u][:, 3, :], nrm[u][:, 1, :]
                c.do(dve.reciprocal(k[:, 12, :], lg[u][:, 2, :]))
                c.do(tt(k[:, 16, :], x2n, r2, ALU.mult))
                c.do(ts(k[:, 17, :], x2n, -1.0, 1.0, ALU.mult, ALU.add))
                for g in range(G):
                    c.do(dve.tensor_tensor_reduce(out=prod_v[:, g, :], in0=xd[u][:, g, :], in1=run[u][:, g, :], scale=1.0,
                                                  scalar=0.0, op0=ALU.mult, op1=ALU.add, accum_out=k[:, 11, g:g + 1]))
                c.settle(but=2 + G)
                c.step(stt(k[:, 12, :], r2, EPS * EPS, k[:, 12, :], ALU.is_gt, ALU.mult))
                dve.wait_ge(s_exp, done(b * S + u))
                c.step(ts(k[:, 13, :], k[:, 10, :], 1.0, None, ALU.add))
                c.do(stt(k[:, 14, :], k[:, 10, :], -1.0, k[:, 12, :], ALU.add, ALU.mult))
                c.step(dve.reciprocal(k[:, 13, :], k[:, 13, :]))
                c.step(tt(k[:, 13, :], k[:, 14, :], k[:, 13, :], ALU.mult))
                c.do(tt(k[:, 14, :], k[:, 13, :], k[:, 13, :], ALU.mult))
                c.do(stt(k[:, 15, :], k[:, 13, :], 2.0, k[:, 11, :], ALU.mult, ALU.mult))
                c.settle()
                c.do(tt(k[:, 16, :], k[:, 16, :], k[:, 14, :], ALU.mult))
                c.do(tt(k[:, 18, :], r2, k[:, 14, :], ALU.mult))
                c.settle()
                c.do(stt(k[:, 16, :], k[:, 15, :], 1.0, k[:, 16, :], ALU.add, ALU.add))
                c.do(tt(k[:, 17, :], k[:, 17, :], k[:, 13, :], ALU.mult))
                c.do(stt(k[:, 18, :], k[:, 15, :], 1.0, k[:, 18, :], ALU.add, ALU.add))
                c.settle()
                c.step(ts(k[:, 16, :], k[:, 16, :], EPS, None, ALU.max))
                c.step(dve.reciprocal(k[:, 19, :], k[:, 16, :]))
                c.do(tt(k[:, 20, :], k[:, 18, :], k[:, 19, :], ALU.mult))
                tt(k[:, 21, :], k[:, 17, :], k[:, 19, :], ALU.mult).then_inc(s_vc, 1)

            def values(b, u):
                k = q[u]
                c.settle()
                c.step(ts(k[:, 20, :], k[:, 20, :], 1.0, None, ALU.add))
                dve.wait_ge(s_vpart, done(b * S + u))
                for g in range(G):
                    c.do(stt(v[u][:, g, :], xd[u][:, g, :], k[:, 20, g:g + 1], v[u][:, g, :], ALU.mult, ALU.add))
                c.settle()
                for g in range(G):
                    c.do(dve.bn_stats(out=st[u][:, g, :], in_=v[u][:, g, :]))
                c.settle()
                for g in range(G):
                    ins = dve.bn_aggr(out=mv[u][:, g, :], in_=st[u][:, g, :])
                ins.then_inc(s_st, 1)

            def bias(b, u):
                dve.wait_ge(s_rs, done(b * S + u))
                stt(rs[u][:, 2, :], mv[u][:, :, 0], -1.0, rs[u][:, 1, :], ALU.mult, ALU.mult).then_inc(s_nb, 1)
                c.restart()

            pipeline(blocks_of(dve, tail), S, dve,
                     [(4, arguments), (1, message_factors), (4, value_factors), (1, messages), (4, values), (3, clip),
                      (2, scan), (4, bias)])


def schnet_edges(nc, a, x2, t_agg, ident, w, w_f1, col, biases, half, one):
    with ExitStack() as ctx:
        sems = []
        ctx.callback(nc.all_engine_barrier)
        ctx.callback(nc.clear_and_free_semaphores, sems)

        def sb(n, shape, dt=F32):
            return ctx.enter_context(nc.sbuf_tensor("se_" + n, shape, dt))

        def sem(n):
            sems.append(nc.alloc_semaphore("se_" + n))
            return sems[-1]

        RG = range(SG)
        ic = [sb(f"ic{u}", [P, 2 * JG], I32) for u in RG]
        wc = [sb(f"wc{u}", [P, JG]) for u in RG]
        ft = [sb(f"ft{u}", [RBF, GE]) for u in RG]
        srow = [sb(f"srow{u}", [P, GE], I32) for u in RG]
        scol = [sb(f"scol{u}", [P, JG]) for u in RG]
        eq = [sb(f"eq{u}", [P, JG, HE]) for u in RG]
        cnt = [sb(f"cnt{u}", [P, JG]) for u in RG]
        idx = [sb(f"idx{u}", [P, JG], I32) for u in RG]
        xg = [sb(f"xg{u}", [P, JG, D]) for u in RG]
        xt = [sb(f"xt{u}", [P, GE]) for u in RG]
        ab = [sb(f"ab{u}", [P, GE]) for u in RG]
        sp_t = [sb(f"sp{u}", [P, GE]) for u in RG]
        bw = [sb(f"bw{u}", [P, JG, D]) for u in RG]
        hb = [sb(f"hb{u}", [P, JG, D]) for u in RG]
        wij = [sb(f"wij{u}", [P, JG, D]) for u in RG]
        msg = [sb(f"msg{u}", [P, JG, D]) for u in RG]
        tot = [sb(f"tot{u}", [P, JG, D]) for u in RG]
        earlier = sb("earlier", [P, JG, HE])
        dummy = sb("dummy", [P, JG])
        dummy_i = sb("dummy_i", [P, JG], I32)
        junk = sb("junk", [P, JG, HE])
        p_t, p_z, p_w, p_h = (ctx.enter_context(nc.psum_tensor(f"se_p{k}", [P, GE], F32)) for k in "tzwh")
        p_s = [ctx.enter_context(nc.psum_tensor(f"se_s{k}", [P, GE], F32)) for k in range(2)]

        cols_in = [sem(f"cols_in{u}") for u in RG]
        rest_in = [sem(f"rest_in{u}") for u in RG]
        gathered = [sem(f"gathered{u}") for u in RG]
        added = [sem(f"added{u}") for u in RG]
        s_tr, s_xt, s_h, s_z, s_ln, s_sp, s_w, s_wij, s_msg, s_eq, s_sum, s_tot, s_idx, s_abs, s_hb = (
            sem(k) for k in ("tr", "xt", "h", "z", "ln", "sp", "w", "wij", "msg", "eq", "sum", "tot", "idx", "abs", "hb"))
        s_dve, s_act, s_pool, s_hold, s_tri = sem("dve"), sem("act"), sem("pool"), sem("hold"), sem("tri")
        IT = GROUPS // SG
        block = ctx.enter_context(nc.Block())

        @block.sync
        def _(sp):
            def load(i, u):
                t = i * SG + u
                if not (isinstance(i, int) and i == 0):
                    held(sp, added[u], i * (16 * JG), s_hold)
                held(sp, s_z, freed(t, SG), s_hold)
                held(sp, s_wij, freed(t, SG), s_hold)
                held(sp, s_eq, freed(t, SG), s_hold)
                held(sp, s_msg, freed(t, SG), s_hold)
                sp.dma_start(ic[u][:], a["e_idx"][bass.ds(t * P, P)]).then_inc(cols_in[u], 16)
                sp.dma_start(wc[u][:], a["e_w"][bass.ds(t * P, P)]).then_inc(rest_in[u], 16)
                sp.dma_start(ft[u][:], a["attr_t"][:, bass.ds(t * GE, GE)]).then_inc(rest_in[u], 16)
                sp.dma_start(srow[u][:], a["src_row"][bass.ds(t, 1)].to_broadcast([P, GE])).then_inc(rest_in[u], 16)

            pipeline(IT, SG, sp, [(0, load)])
            for u in RG:
                held(sp, added[u], 16 * JG * IT, s_hold)

        @block.gpsimd
        def _(pool):
            c = Steps(pool, s_pool)
            c.step(pool.memset(earlier[:], 1.0))
            for j in range(JG):
                ins = pool.affine_select(out=earlier[:, j, :], in_=earlier[:, j, :], compare_op=ALU.is_gt, fill=0.0,
                                         base=P * (j % JH), pattern=[[-1, HE]], channel_multiplier=1)
            ins.then_inc(s_tri, 1)
            pool.iota(dummy_i[:], pattern=[[P, JG]], base=DUMMY, channel_multiplier=1).then_inc(s_tri, 1)

            def gather(i, u, half):
                if half == 0:
                    held(pool, cols_in[u], i * 16 + 16, s_hold)
                for j in range(half * JH, (half + 1) * JH):
                    pool.indirect_dma_start(out=xg[u][:, j, :], out_offset=None, in_=x2,
                                            in_offset=bass.IndirectOffsetOnAxis(ap=ic[u][:, j:j + 1], axis=0),
                                            bounds_check=N - 1, oob_is_err=False).then_inc(gathered[u], 16)

            def add(i, u, half):
                if half == 0:
                    held(pool, s_idx, done(i * SG + u), s_hold)
                    held(pool, s_tot, done(i * SG + u), s_hold)
                if half == 1:
                    held(pool, added[u], i * (16 * JG) + 16 * JH, s_hold)
                elif u > 0:
                    held(pool, added[u - 1], i * (16 * JG) + 16 * JG, s_hold)
                elif not (isinstance(i, int) and i == 0):
                    held(pool, added[SG - 1], i * (16 * JG), s_hold)
                for j in range(half * JH, (half + 1) * JH):
                    pool.indirect_dma_start(out=t_agg, out_offset=bass.IndirectOffsetOnAxis(ap=idx[u][:, j:j + 1], axis=0),
                                            in_=tot[u][:, j, :], in_offset=None,
                                            bounds_check=AGG_ROWS - 1, oob_is_err=True,
                                            compute_op=ALU.add).then_inc(added[u], 16)

            pipeline(IT, SG, pool, [(3, lambda i, u: add(i, u, 0)), (0, lambda i, u: gather(i, u, 0)),
                                    (3, lambda i, u: add(i, u, 1)), (0, lambda i, u: gather(i, u, 1))])

        @block.tensor
        def _(pe):
            for s in (s_tr, s_h, s_z, s_w, s_sum):
                pe.sem_inc(s, CREDIT)

            def filters(i, u):
                t = i * SG + u
                pe.wait_ge(rest_in[u], i * 48 + 48)
                pe.wait_ge(s_sp, freed(t, 1))
                pe.wait_ge(s_abs, freed(t, 1))
                pe.matmul(p_z[:], w_f1[:], ft[u][:], start=True, stop=True).then_inc(s_z, 1)
                pe.wait_ge(gathered[u], i * (16 * JG) + 16 * JG)
                pe.wait_ge(s_xt, freed(t, 1))
                for j in range(JG):
                    ins = pe.transpose(p_t[:, j * P:(j + 1) * P], xg[u][:, j, :], ident[:])
                ins.then_inc(s_tr, 1)

            def products(i, u):
                t = i * SG + u
                pe.wait_ge(s_xt, done(t))
                pe.wait_ge(s_hb, freed(t, 1))
                for j in range(JG):
                    ins = pe.matmul(p_h[:, j * D:(j + 1) * D], xt[u][:, j * P:(j + 1) * P], w["in2f"][:],
                                    start=True, stop=True)
                ins.then_inc(s_h, 1)
                pe.wait_ge(s_sp, done(t))
                pe.wait_ge(s_wij, freed(t, 1))
                for j in range(JG):
                    ins = pe.matmul(p_w[:, j * D:(j + 1) * D], sp_t[u][:, j * P:(j + 1) * P], w["f2"][:],
                                    start=True, stop=True)
                ins.then_inc(s_w, 1)

            def sums(i, u):
                t = i * SG + u
                pe.wait_ge(s_eq, done(t))
                pe.wait_ge(s_msg, done(t))
                pe.wait_ge(s_tot, freed(t, 2))
                for j in range(JG):
                    for k in range(JH):
                        ins = pe.matmul(p_s[u % 2][:, j * D:(j + 1) * D], eq[u][:, j // JH * JH + k, j % JH * P:(j % JH + 1) * P],
                                        msg[u][:, j // JH * JH + k, :], start=(k == 0), stop=(k == JH - 1))
                ins.then_inc(s_sum, 1)

            pipeline(IT, SG, pe, [(1, products), (2, sums), (0, filters)])

        @block.scalar
        def _(act):
            act.preload_act_table_set("natural_log_exp_and_others")
            c = Steps(act, s_act)
            for s in (s_xt, s_ln, s_wij, s_tot, s_abs):
                act.sem_inc(s, CREDIT)

            def softplus(i, u):
                t = i * SG + u
                act.wait_ge(s_z, done(t))
                act.wait_ge(s_sp, freed(t, SG))
                act.activation(ab[u][:], p_z[:], ACT.Abs, bias=col[:, 0:1]).then_inc(s_abs, 1)
                act.wait_ge(s_abs, done(t))
                c.step(act.activation(ab[u][:], ab[u][:], ACT.Exp, scale=-1.0))
                act.activation(ab[u][:], ab[u][:], ACT.Ln, bias=half, scale=0.5).then_inc(s_ln, 1)
                act.wait_ge(s_tr, done(t))
                act.wait_ge(s_h, freed(t, SG))
                act.activation(xt[u][:], p_t[:], ACT.Copy).then_inc(s_xt, 1)

            def weigh(i, u):
                t = i * SG + u
                act.wait_ge(s_w, done(t))
                act.wait_ge(s_msg, freed(t, SG))
                for j in range(JG):
                    ins = act.activation(wij[u][:, j, :], p_w[:, j * D:(j + 1) * D], ACT.Copy, scale=wc[u][:, j:j + 1])
                ins.then_inc(s_wij, 1)
                c.restart()

            def totals(i, u):
                t = i * SG + u
                act.wait_ge(s_sum, done(t))
                act.wait_ge(cols_in[u], i * 16 + 16)
                act.activation(tot[u][:].rearrange("p j d -> p (j d)"), p_s[u % 2][:], ACT.Copy).then_inc(s_tot, 1)

            pipeline(IT, SG, act, [(1, weigh), (2, totals), (0, softplus)])

        @block.vector
        def _(dve):
            c = Steps(dve, s_dve)
            for s in (s_sp, s_msg, s_eq, s_idx, s_hb):
                dve.sem_inc(s, CREDIT)
            dve.wait_ge(s_tri, 2)
            c.step(dve.tensor_copy(dummy[:], dummy_i[:]))

            def equal(i, u):
                t = i * SG + u
                dve.wait_ge(rest_in[u], i * 48 + 48)
                dve.wait_ge(cols_in[u], i * 16 + 16)
                dve.wait_ge(s_sum, freed(t, SG))
                c.step(dve.tensor_copy(scol[u][:], ic[u][:, JG:2 * JG]))
                for k in range(JG):
                    ins = dve.tensor_scalar(eq[u][:, k, :], srow[u][:, k // JH * HE:(k // JH + 1) * HE], scol[u][:, k:k + 1], None, ALU.is_equal)
                ins.then_inc(s_eq, 1)

            def weighted_bias(i, u):
                t = i * SG + u
                dve.wait_ge(rest_in[u], i * 48 + 48)
                dve.wait_ge(s_msg, freed(t, SG))
                c.do(dve.tensor_tensor(bw[u][:], over_rows(biases[:, 1, :], JG), lanes_of(wc[u][:], JG), ALU.mult))

            def hidden_bias(i, u):
                t = i * SG + u
                dve.wait_ge(s_h, done(t))
                dve.wait_ge(s_msg, freed(t, SG))
                dve.tensor_tensor(hb[u][:], p_h[:].rearrange("p (j d) -> p j d", j=JG), over_rows(biases[:, 0, :], JG),
                                  ALU.add).then_inc(s_hb, 1)

            def softplus_sum(i, u):
                t = i * SG + u
                dve.wait_ge(s_abs, done(t))
                dve.wait_ge(s_w, freed(t, SG))
                c.step(dve.tensor_scalar(sp_t[u][:], p_z[:], col[:, 0:1], 0.0, ALU.add, ALU.max))
                dve.wait_ge(s_ln, done(t))
                dve.tensor_tensor(sp_t[u][:], sp_t[u][:], ab[u][:], ALU.add).then_inc(s_sp, 1)

            def first(i, u):
                t = i * SG + u
                dve.wait_ge(s_eq, done(t))
                dve.wait_ge(cols_in[u], i * 16 + 16)
                for k in range(JG):
                    c.do(dve.tensor_tensor_reduce(out=junk[:, k, :], in0=eq[u][:, k, :], in1=earlier[:, k, :], scale=1.0,
                                                  scalar=0.0, op0=ALU.mult, op1=ALU.add, accum_out=cnt[u][:, k:k + 1]))
                c.settle()
                c.do(dve.tensor_scalar(cnt[u][:], cnt[u][:], 0.5, None, ALU.is_lt))
                c.step(dve.tensor_tensor(scol[u][:], scol[u][:], dummy[:], ALU.subtract))
                c.step(dve.tensor_tensor(scol[u][:], scol[u][:], cnt[u][:], ALU.mult))
                dve.tensor_tensor(idx[u][:], scol[u][:], dummy[:], ALU.add).then_inc(s_idx, 1)

            def messages(i, u):
                t = i * SG + u
                dve.wait_ge(s_wij, done(t))
                dve.wait_ge(s_sum, freed(t, SG))
                dve.wait_ge(s_hb, done(t))
                c.step(dve.tensor_tensor(bw[u][:], bw[u][:], wij[u][:], ALU.add))
                dve.tensor_tensor(msg[u][:], hb[u][:], bw[u][:], ALU.mult).then_inc(s_msg, 1)
                c.restart()

            c.restart()
            pipeline(IT, SG, dve, [(1, hidden_bias), (1, messages), (0, softplus_sum), (0, equal), (0, first), (0, weighted_bias)])


def schnet_nodes(nc, x2, t_agg, x3, out, ident, w, col, bias_o2, half):
    with ExitStack() as ctx:
        sems = []
        ctx.callback(nc.all_engine_barrier)
        ctx.callback(nc.clear_and_free_semaphores, sems)

        def sb(n, shape, dt=F32):
            return ctx.enter_context(nc.sbuf_tensor("sn_" + n, shape, dt))

        def sem(n):
            sems.append(nc.alloc_semaphore("sn_" + n))
            return sems[-1]

        R4 = range(SN)
        xi = [sb(f"x{u}", [P, NB, D]) for u in R4]
        ag = [sb(f"agg{u}", [P, NB, D]) for u in R4]
        at = [sb(f"at{u}", [P, BN]) for u in R4]
        ab = [sb(f"ab{u}", [P, BN]) for u in R4]
        sp_t = [sb(f"sp{u}", [P, BN]) for u in R4]
        v = [sb(f"v{u}", [P, NB, D]) for u in R4]
        st = [sb(f"st{u}", [P, NB, 6]) for u in R4]
        mv = [sb(f"mv{u}", [P, NB, 2]) for u in R4]
        rs = [sb(f"rs{u}", [P, 3, NB]) for u in R4]
        arg = [sb(f"arg{u}", [P, 3, NB]) for u in R4]
        o = [sb(f"o{u}", [P, NB, D]) for u in R4]
        o2 = [sb(f"o2{u}", [P, NB, D]) for u in R4]
        p_t, p_z, p_o = ([ctx.enter_context(nc.psum_tensor(f"sn_p{k}{m}", [P, BN], F32)) for m in range(2)] for k in "tzo")
        agg_in = [sem(f"agg_in{u}") for u in R4]
        x_in = [sem(f"x_in{u}") for u in R4]
        stored = [sem(f"stored{u}") for u in R4]
        s_tr, s_at, s_z, s_abs, s_ln, s_sp, s_mm, s_v, s_st, s_rs, s_nb, s_o, s_o2, s_xb = (
            sem(k) for k in ("tr", "at", "z", "abs", "ln", "sp", "mm", "v", "st", "rs", "nb", "o", "o2", "xb"))
        s_dve, s_act, s_hold = sem("dve"), sem("act"), sem("hold")
        IT = BATCHES // SN
        block = ctx.enter_context(nc.Block())

        @block.sync
        def _(sp):
            def load_agg(i, u):
                t = i * SN + u
                held(sp, s_tr, freed(t, SN), s_hold)
                sp.dma_start(flat(ag[u]), node_view(t_agg, t)).then_inc(agg_in[u], 16)

            def load_x(i, u):
                t = i * SN + u
                held(sp, s_v, freed(t, SN), s_hold)
                sp.dma_start(flat(xi[u]), node_view(x2, t)).then_inc(x_in[u], 16)

            pipeline(IT, SN, sp, [(0, load_agg), (3, load_x)])

        @block.tensor
        def _(pe):
            for s in (s_tr, s_z, s_mm):
                pe.sem_inc(s, CREDIT)

            def transposes(i, u):
                t = i * SN + u
                pe.wait_ge(agg_in[u], i * 16 + 16)
                pe.wait_ge(s_at, freed(t, 2))
                for j in range(NB):
                    ins = pe.transpose(p_t[u % 2][:, j * P:(j + 1) * P], ag[u][:, j, :], ident[:])
                ins.then_inc(s_tr, 1)

            def hidden(i, u):
                t = i * SN + u
                pe.wait_ge(s_at, done(t))
                pe.wait_ge(s_abs, freed(t, 2))
                pe.wait_ge(s_sp, freed(t, 2))
                pe.matmul(p_z[u % 2][:], w["o1"][:], at[u][:], start=True, stop=True).then_inc(s_z, 1)

            def outputs(i, u):
                t = i * SN + u
                pe.wait_ge(s_sp, done(t))
                pe.wait_ge(s_v, freed(t, 2))
                for j in range(NB):
                    ins = pe.matmul(p_o[u % 2][:, j * D:(j + 1) * D], sp_t[u][:, j * P:(j + 1) * P], w["o2"][:],
                                    start=True, stop=True)
                ins.then_inc(s_mm, 1)

            pipeline(IT, SN, pe, [(4, outputs), (0, transposes), (1, hidden)])

        @block.scalar
        def _(act):
            act.preload_act_table_set("natural_log_exp_and_others")
            c = Steps(act, s_act)
            for s in (s_at, s_abs, s_ln, s_rs, s_o, *stored):
                act.sem_inc(s, CREDIT)

            def copy(i, u):
                t = i * SN + u
                act.wait_ge(s_tr, done(t))
                act.wait_ge(s_z, freed(t, SN))
                act.activation(at[u][:], p_t[u % 2][:], ACT.Copy).then_inc(s_at, 1)

            def softplus(i, u):
                t = i * SN + u
                act.wait_ge(s_z, done(t))
                act.wait_ge(s_sp, freed(t, SN))
                act.activation(ab[u][:], p_z[u % 2][:], ACT.Abs, bias=col[:, 1:2]).then_inc(s_abs, 1)
                act.wait_ge(s_abs, done(t))
                c.step(act.activation(ab[u][:], ab[u][:], ACT.Exp, scale=-1.0))
                act.activation(ab[u][:], ab[u][:], ACT.Ln, bias=half, scale=0.5).then_inc(s_ln, 1)
                c.restart()

            def roots(i, u):
                t = i * SN + u
                act.wait_ge(s_st, done(t))
                act.wait_ge(s_o2, freed(t, SN))
                norm_factors_root(act, c, arg[u], rs[u]).then_inc(s_rs, 1)
                c.restart()

            def norm(i, u):
                act.wait_ge(s_nb, done(i * SN + u))
                act.wait_ge(stored[u], i * 32 + CREDIT)
                for j in range(NB):
                    ins = act.activation(o[u][:, j, :], v[u][:, j, :], ACT.Identity, bias=rs[u][:, 2, j:j + 1], scale=rs[u][:, 0, j:j + 1])
                ins.then_inc(s_o, 1)

            def store(i, u):
                t = i * SN + u
                act.wait_ge(s_o, done(t))
                act.dma_start(node_view(x3, t), flat(o[u])).then_inc(stored[u], 16)
                act.wait_ge(s_o2, done(t))
                act.dma_start(node_view(out, t), flat(o2[u])).then_inc(stored[u], 16)

            pipeline(IT, SN, act, [(2, softplus), (0, copy), (8, norm), (9, store), (6, roots)])
            for u in R4:
                act.wait_ge(stored[u], 32 * IT + CREDIT)

        @block.vector
        def _(dve):
            c = Steps(dve, s_dve)
            for s in (s_sp, s_v, s_st, s_nb):
                dve.sem_inc(s, CREDIT)

            def softplus_sum(i, u):
                t = i * SN + u
                dve.wait_ge(s_abs, done(t))
                dve.wait_ge(s_mm, freed(t, SN))
                c.step(dve.tensor_scalar(sp_t[u][:], p_z[u % 2][:], col[:, 1:2], 0.0, ALU.add, ALU.max))
                dve.wait_ge(s_ln, done(t))
                dve.tensor_tensor(sp_t[u][:], sp_t[u][:], ab[u][:], ALU.add).then_inc(s_sp, 1)

            def values(i, u):
                t = i * SN + u
                dve.wait_ge(s_mm, done(t))
                dve.wait_ge(s_xb, done(t))
                dve.wait_ge(s_o, freed(t, SN))
                dve.tensor_tensor(flat(v[u]), p_o[u % 2][:], flat(xi[u]), ALU.add).then_inc(s_v, 1)
                dve.wait_ge(s_v, done(t))
                norm_factors_begin(dve, c, v[u], st[u], mv[u], arg[u]).then_inc(s_st, 1)
                c.restart()

            def bias(i, u):
                dve.wait_ge(s_rs, done(i * SN + u))
                dve.scalar_tensor_tensor(rs[u][:, 2, :], mv[u][:, :, 0], -1.0, rs[u][:, 0, :], ALU.mult, ALU.mult).then_inc(s_nb, 1)

            pipeline(IT, SN, dve, [(3, softplus_sum), (5, values), (7, bias)])

        @block.gpsimd
        def _(pool):
            pool.sem_inc(s_o2, CREDIT)
            pool.sem_inc(s_xb, CREDIT)

            def residual(i, u):
                held(pool, x_in[u], i * 16 + 16, s_hold)
                pool.tensor_tensor(xi[u][:], xi[u][:], over_rows(bias_o2, NB), ALU.add).then_inc(s_xb, 1)

            def double(i, u):
                held(pool, s_o, done(i * SN + u), s_hold)
                held(pool, stored[u], i * 32 + CREDIT, s_hold)
                pool.tensor_tensor(o2[u][:], o[u][:], lanes_of(rs[u][:, 1, :], NB), ALU.mult).then_inc(s_o2, 1)

            pipeline(IT, SN, pool, [(4, residual), (8, double)])


def last_pass(nc, meta, tail, x3, out, ident, w, bias3, consts):
    with ExitStack() as ctx:
        sems = []
        ctx.callback(nc.all_engine_barrier)
        ctx.callback(nc.clear_and_free_semaphores, sems)

        def sb(n, shape, dt=F32):
            return ctx.enter_context(nc.sbuf_tensor("last_" + n, shape, dt))

        def sem(n):
            sems.append(nc.alloc_semaphore("last_" + n))
            return sems[-1]

        mt = [sb(f"mt{u}", [P, FIELDS, G], I32) for u in range(S)]
        mf = [t[:].bitcast(F32) for t in mt]
        msg, xd, run, row, v, o = ([sb(f"{n}{u}", [P, G, D]) for u in range(S)] for n in ("msg", "xd", "run", "row", "v", "o"))
        xt, rt = sb("xt", [P, G * P]), sb("rt", [P, G * P])
        st = [sb(f"st{u}", [P, G, 6]) for u in range(S)]
        mv = [sb(f"mv{u}", [P, G, 2]) for u in range(S)]
        rs = [sb(f"rs{u}", [P, 3, G]) for u in range(S)]
        p_x, p_r, p_z = (ctx.enter_context(nc.psum_tensor(f"last_{n}", [P, G * D], F32)) for n in "xrz")
        meta_in, gathered, scattered = ([sem(f"{n}{u}") for u in range(S)] for n in ("meta_in", "gathered", "scattered"))
        s_sum, s_row, s_tr, s_t, s_mm, s_z, s_st, s_rs, s_nb, s_o = (
            sem(n) for n in ("sum", "row", "tr", "t", "mm", "z", "st", "rs", "nb", "o"))
        s_dve, s_act, s_hold = sem("dve"), sem("act"), sem("hold")
        eps_ln = consts[:, 0:1]
        block = ctx.enter_context(nc.Block())

        def step(b, u):
            return b * S + u

        @block.sync
        def _(sp):
            n = blocks_of(sp, tail)
            pipeline(n, S, sp, [(0, lambda b, u: load_meta(sp, mt, meta, b, u, scattered, meta_in, s_hold))])
            for u in range(S):
                held(sp, scattered[u], n * (16 * G), s_hold)

        @block.gpsimd
        def _(pool):
            def gather(b, u):
                held(pool, meta_in[u], b * 48 + 48, s_hold)
                gather_rows(pool, x3, mt[u], SRC, msg[u], gathered[u])
                gather_rows(pool, x3, mt[u], DST, xd[u], gathered[u])

            def scatter(b, u):
                held(pool, s_o, done(step(b, u)), s_hold)
                scatter_rows(pool, out, mt[u], o[u], scattered[u])

            pipeline(blocks_of(pool, tail), S, pool, [(0, gather), (3, scatter)])

        @block.tensor
        def _(pe):
            for s in (s_tr, s_mm):
                pe.sem_inc(s, CREDIT)

            def transposes(b, u):
                pe.wait_ge(gathered[u], b * (32 * G) + 32 * G)
                pe.wait_ge(s_row, done(step(b, u)))
                pe.wait_ge(s_t, freed(step(b, u), 1))
                for src, bank in ((xd, p_x), (row, p_r)):
                    for g in range(G):
                        ins = pe.transpose(bank[:, g * P:(g + 1) * P], src[u][:, g, :], ident[:])
                ins.then_inc(s_tr, 1)

            def products(b, u):
                pe.wait_ge(s_t, done(step(b, u)))
                pe.wait_ge(s_z, freed(step(b, u), 1))
                for g in range(G):
                    pe.matmul(p_z[:, g * D:(g + 1) * D], xt[:, g * P:(g + 1) * P], w["h3"][:], start=True, stop=False)
                    ins = pe.matmul(p_z[:, g * D:(g + 1) * D], rt[:, g * P:(g + 1) * P], w["c3"][:], start=False, stop=True)
                ins.then_inc(s_mm, 1)

            pipeline(blocks_of(pe, tail), S, pe, [(1, transposes), (1, products)])

        @block.scalar
        def _(act):
            act.preload_act_table_set("natural_log_exp_and_others")
            c = Steps(act, s_act)
            for s in (s_row, s_t, s_rs, s_o):
                act.sem_inc(s, CREDIT)

            def copies(b, u):
                act.wait_ge(s_tr, done(step(b, u)))
                act.wait_ge(s_mm, freed(step(b, u), 1))
                act.activation(xt[:], p_x[:], ACT.Copy)
                act.activation(rt[:], p_r[:], ACT.Copy).then_inc(s_t, 1)

            def scale(b, u):
                act.wait_ge(s_sum, done(step(b, u)))
                act.wait_ge(s_tr, freed(step(b, u), S))
                for g in range(G):
                    ins = act.activation(row[u][:, g, :], run[u][:, g, :], ACT.Copy, scale=mf[u][:, RDEG, g:g + 1])
                ins.then_inc(s_row, 1)

            def rstd(b, u):
                act.wait_ge(s_st, done(step(b, u)))
                c.step(act.activation(rs[u][:, 0, :], mv[u][:, :, 1], ACT.Ln, bias=eps_ln))
                act.activation(rs[u][:, 1, :], rs[u][:, 0, :], ACT.Exp, scale=-0.5).then_inc(s_rs, 1)
                c.restart()

            def norm(b, u):
                act.wait_ge(s_nb, done(step(b, u)))
                act.wait_ge(meta_in[u], b * 48 + 48)
                for g in range(G):
                    ins = act.activation(o[u][:, g, :], v[u][:, g, :], ACT.Identity, bias=rs[u][:, 2, g:g + 1], scale=rs[u][:, 1, g:g + 1])
                ins.then_inc(s_o, 1)

            pipeline(blocks_of(act, tail), S, act, [(1, copies), (0, scale), (2, norm), (1, rstd)])

        @block.vector
        def _(dve):
            c = Steps(dve, s_dve)
            dve.memset(run[S - 1][:], 0.0).then_inc(s_sum, CREDIT)
            for s in (s_z, s_st, s_nb):
                dve.sem_inc(s, CREDIT)

            def sums(b, u):
                dve.wait_ge(gathered[u], b * (32 * G) + 32 * G)
                dve.wait_ge(s_row, freed(step(b, u), S))
                dve.wait_ge(s_sum, done(step(b, u) - 1))
                for g in range(G):
                    ins = dve.scalar_tensor_tensor(run[u][:, g, :], run[u - 1][:, g, :], mf[u][:, CONT, g:g + 1],
                                                   msg[u][:, g, :], ALU.mult, ALU.add)
                ins.then_inc(s_sum, 1)

            def values(b, u):
                dve.wait_ge(s_mm, done(step(b, u)))
                dve.wait_ge(s_o, freed(step(b, u), S))
                dve.tensor_tensor(v[u][:], p_z[:].rearrange("p (g d) -> p g d", g=G), over_rows(bias3, G),
                                  ALU.add).then_inc(s_z, 1)
                dve.wait_ge(s_z, done(step(b, u)))
                c.step(dve.scalar_tensor_tensor(v[u][:], v[u][:], 0.0, xd[u][:], ALU.max, ALU.add))
                for g in range(G):
                    c.do(dve.bn_stats(out=st[u][:, g, :], in_=v[u][:, g, :]))
                c.settle()
                for g in range(G):
                    ins = dve.bn_aggr(out=mv[u][:, g, :], in_=st[u][:, g, :])
                ins.then_inc(s_st, 1)
                c.restart()

            def bias(b, u):
                dve.wait_ge(s_rs, done(step(b, u)))
                dve.scalar_tensor_tensor(rs[u][:, 2, :], mv[u][:, :, 0], -1.0, rs[u][:, 1, :], ALU.mult,
                                         ALU.mult).then_inc(s_nb, 1)

            pipeline(blocks_of(dve, tail), S, dve, [(2, bias), (0, sums), (1, values)])


def kernel(**inputs):
    import numpy as np
    import concourse.bacc as bacc
    from concourse.bass_utils import run_bass_kernel_spmd

    def t(name):
        return np.ascontiguousarray(np.asarray(inputs[name]).T)

    def arr(name):
        return np.asarray(inputs[name])

    src, dst = arr("src"), arr("dst")
    EG = GROUPS * GE
    src_g = np.full(EG, AGG_ROWS - 1, np.int32)
    src_g[:E] = src
    dst_g = np.zeros(EG, np.int32)
    dst_g[:E] = dst
    w_g = np.zeros(EG, np.float32)
    w_g[:E] = arr("edge_weight")
    attr = np.zeros((RBF, EG), np.float32)
    attr[:, :E] = arr("edge_attr_20").T
    dst_pad = np.full(E_PAD, -1, np.int32)
    dst_pad[0] = -2
    dst_pad[1:E + 1] = dst
    src_pad = np.zeros(E_PAD, np.int32)
    src_pad[:E] = src
    x_pad = np.zeros((NP, D), np.float32)
    x_pad[:N] = arr("x")

    def columns(v):
        return v.reshape(GROUPS, JG, P).transpose(0, 2, 1).reshape(GROUPS * P, JG)

    arrays = {
        "x": x_pad, "dst_pad": dst_pad, "src_pad": src_pad,
        "e_idx": np.concatenate([columns(dst_g), columns(src_g)], axis=1), "e_w": columns(w_g),
        "attr_t": attr, "src_row": src_g.reshape(GROUPS, GE),
        "s0": arr("L0_gnn_W_self0"), "n0": arr("L0_gnn_W_neigh0"),
        "s0t": t("L0_gnn_W_self0"), "n0t": t("L0_gnn_W_neigh0"),
        "s1t": t("L0_gnn_W_self1"), "n1t": t("L0_gnn_W_neigh1"),
        "b_self0": arr("L0_gnn_b_self0"), "b_self1": arr("L0_gnn_b_self1"),
        "w_in2f": t("L2_gnn_W_in2f"), "w_f1": t("L2_gnn_W_f1"), "w_f2": t("L2_gnn_W_f2"),
        "w_o1": t("L2_gnn_W_o1"), "w_o2": t("L2_gnn_W_o2"),
        "w_h3": arr("L3_gnn_W")[0:D], "w_c3": arr("L3_gnn_W")[D:2 * D],
        "b_in2f": arr("L2_gnn_b_in2f"), "b_f1": arr("L2_gnn_b_f1"), "b_f2": arr("L2_gnn_b_f2"),
        "b_o1": arr("L2_gnn_b_o1"), "b_o2": arr("L2_gnn_b_o2"), "b_3": arr("L3_gnn_b"),
    }
    nc = bacc.Bacc("TRN2", target_bir_lowering=False, num_devices=1)
    feeds, aps = {}, {}
    for name, value in arrays.items():
        value = np.ascontiguousarray(value)
        feeds["in_" + name] = value
        aps[name] = nc.dram_tensor("in_" + name, value.shape, mybir.dt.from_np(value.dtype), kind="ExternalInput").ap()
    out = nc.dram_tensor("out_nodes", [NP, D], F32, kind="ExternalOutput").ap()
    gnn_kernel(nc, aps, out)
    result = run_bass_kernel_spmd(nc, [feeds], core_ids=[0])
    return result.results[0]["out_nodes"][:N]
```
